# Optimizing a Trainium2 kernel written in Bass

```python
import numpy as np
import jax
import jax.numpy as jnp

def _softmax(x, axis=-1):
    return jax.nn.softmax(x, axis=axis)

def _gelu(x):
    return jax.nn.gelu(x, approximate=True)

def _silu(x):
    return jax.nn.silu(x)

def _sigmoid(x):
    return jax.nn.sigmoid(x)

def _layernorm(x, axis=-1, eps=1e-05):
    m = jnp.mean(x, axis=axis, keepdims=True)
    v = jnp.var(x, axis=axis, keepdims=True)
    return (x - m) / jnp.sqrt(v + eps)

def _scatter_add(tgt, idx, src, axis=0):
    return tgt.at[idx].add(src)

def _segment_sum(src, seg, n):
    return jax.ops.segment_sum(src, seg, n)
kernel_name = 'mk_xattn_seq_d2_seqx_r8_3ed397'

def setup_inputs(seed: int=0):
    np.random.seed(seed)
    _w = jnp.asarray

    def _rec_inputs():
        import jax
        import jax.numpy as jnp
        _rk = jax.random.key(seed)
        x = -0.0001108 + 0.9999 * jax.random.normal(jax.random.fold_in(_rk, 1), (8, 256, 160), jnp.float32)
        _lenS = 256 - jax.random.randint(jax.random.fold_in(_rk, 7), (8,), 0, max(1, 256 // 4) + 1, jnp.int32)
        _lenS2 = 1601 - jax.random.randint(jax.random.fold_in(_rk, 8), (8,), 0, max(1, 1601 // 4) + 1, jnp.int32)
        _ctx_768P = jax.random.normal(jax.random.fold_in(_rk, 11), (8, 16, 96), jnp.float32)
        _ctx_768c = jax.random.dirichlet(jax.random.fold_in(_rk, 511), 0.3 * jnp.ones((16,), jnp.float32), (8, 1601))
        _ctx_768t = jnp.einsum('bsk,bkd->bsd', _ctx_768c, _ctx_768P)
        _ctx_768t = _ctx_768t * jax.lax.rsqrt(jnp.mean(jnp.square(_ctx_768t)) + 1e-12) * 0.953939
        ctx_768 = 0.000364016 + 1.0001 * (_ctx_768t + 0.3 * jax.random.normal(jax.random.fold_in(_rk, 611), (8, 1601, 96), jnp.float32))
        return (x, ctx_768)
    x, ctx_768 = _rec_inputs()

    def _L0_xattn_setup():
        import jax, jax.numpy as jnp
        import numpy as np
        B, S, D = (32, 128, 160)
        CROSS = 96
        HEADS = 20
        HD = D // HEADS
        N_AOE, N_IMG = (16, 16)
        SCALE = 1.0 / float(np.sqrt(HD))

        def _split_heads(x):
            b, n, _ = x.shape
            return x.reshape(b, n, HEADS, HD).transpose(0, 2, 1, 3)

        def _attend(q, k, v):
            scores = jnp.einsum('bhsd,bhkd->bhsk', q, k) * SCALE
            probs = jax.nn.softmax(scores, axis=-1)
            return jnp.einsum('bhsk,bhkd->bhsd', probs, v)
        key = jax.random.key(seed)
        ks = jax.random.split(key, 10)
        g = lambda k, shape, sc=0.02: jax.random.normal(k, shape, jnp.float32) * sc
        return {'hidden_states': jax.random.normal(ks[0], (B, S, D), jnp.float32), 'encoder_hidden_states': jax.random.normal(ks[1], (B, N_AOE + N_IMG + 16, CROSS), jnp.float32), 'w_q': g(ks[2], (D, D)), 'w_k': g(ks[3], (D, CROSS)), 'w_v': g(ks[4], (D, CROSS)), 'w_k_dis': g(ks[5], (D, CROSS)), 'w_v_dis': g(ks[6], (D, CROSS)), 'w_gate': g(ks[7], (1, CROSS)), 'b_gate': jnp.zeros((1,), jnp.float32), 'anat_gate_logit': jnp.float32(0.0), 'dis_gate_logit': jnp.float32(0.0), 'w_out': g(ks[8], (D, D)), 'b_out': jnp.zeros((D,), jnp.float32)}
    _L0_xattn_all = _L0_xattn_setup()
    _L0_xattn_in = {k: v for k, v in _L0_xattn_all.items() if k in ('w_q', 'w_k', 'w_v', 'w_k_dis', 'w_v_dis', 'w_gate', 'b_gate', 'anat_gate_logit', 'dis_gate_logit', 'w_out', 'b_out')}
    del _L0_xattn_all

    def _L1_xattn_setup():
        import jax, jax.numpy as jnp
        import numpy as np
        HEADS = 8
        NUM_TOKENS = 4
        CROSS_ATTENTION_DIM = 96

        def _mha(q, k, v, heads=HEADS):
            B, Sq, H = q.shape
            Sk = k.shape[1]
            d = H // heads
            qh = q.reshape(B, Sq, heads, d).transpose(0, 2, 1, 3)
            kh = k.reshape(B, Sk, heads, d).transpose(0, 2, 1, 3)
            vh = v.reshape(B, Sk, heads, d).transpose(0, 2, 1, 3)
            scores = jnp.einsum('bhqd,bhkd->bhqk', qh, kh) * jnp.asarray(d, q.dtype) ** (-0.5)
            probs = jax.nn.softmax(scores, axis=-1)
            out = jnp.einsum('bhqk,bhkd->bhqd', probs, vh)
            return out.transpose(0, 2, 1, 3).reshape(B, Sq, H)
        key = jax.random.key(seed)
        ks = jax.random.split(key, 10)
        B, S, H, CAD, T = (4, 128, 160, CROSS_ATTENTION_DIM, NUM_TOKENS)
        sc = 0.02
        return {'hidden_states': jax.random.normal(ks[0], (B, S, H), jnp.float32), 'encoder_hidden_states': jax.random.normal(ks[1], (B, 77 + T, CAD), jnp.float32), 'Wq': jax.random.normal(ks[2], (H, H), jnp.float32) * sc, 'Wk': jax.random.normal(ks[3], (CAD, H), jnp.float32) * sc, 'Wv': jax.random.normal(ks[4], (CAD, H), jnp.float32) * sc, 'Wq_ca': jax.random.normal(ks[5], (T, H), jnp.float32) * sc, 'Wk_ca': jax.random.normal(ks[6], (CAD, H), jnp.float32) * sc, 'Wv_ca': jax.random.normal(ks[7], (CAD, H), jnp.float32) * sc, 'Wout': jax.random.normal(ks[8], (H, H), jnp.float32) * sc, 'b_out': jnp.zeros((H,), jnp.float32)}
    _L1_xattn_all = _L1_xattn_setup()
    _L1_xattn_in = {k: v for k, v in _L1_xattn_all.items() if k in ('Wq', 'Wk', 'Wv', 'Wq_ca', 'Wk_ca', 'Wv_ca', 'Wout', 'b_out')}
    del _L1_xattn_all
    return {'x': x, 'ctx_768': ctx_768, 'L0_xattn_w_q': _L0_xattn_in['w_q'], 'L0_xattn_w_k': _L0_xattn_in['w_k'], 'L0_xattn_w_v': _L0_xattn_in['w_v'], 'L0_xattn_w_k_dis': _L0_xattn_in['w_k_dis'], 'L0_xattn_w_v_dis': _L0_xattn_in['w_v_dis'], 'L0_xattn_w_gate': _L0_xattn_in['w_gate'], 'L0_xattn_b_gate': _L0_xattn_in['b_gate'], 'L0_xattn_anat_gate_logit': _L0_xattn_in['anat_gate_logit'], 'L0_xattn_dis_gate_logit': _L0_xattn_in['dis_gate_logit'], 'L0_xattn_w_out': _L0_xattn_in['w_out'], 'L0_xattn_b_out': _L0_xattn_in['b_out'], 'L1_xattn_Wq': _L1_xattn_in['Wq'], 'L1_xattn_Wk': _L1_xattn_in['Wk'], 'L1_xattn_Wv': _L1_xattn_in['Wv'], 'L1_xattn_Wq_ca': _L1_xattn_in['Wq_ca'], 'L1_xattn_Wk_ca': _L1_xattn_in['Wk_ca'], 'L1_xattn_Wv_ca': _L1_xattn_in['Wv_ca'], 'L1_xattn_Wout': _L1_xattn_in['Wout'], 'L1_xattn_b_out': _L1_xattn_in['b_out']}

def reference(x, ctx_768, L0_xattn_w_q, L0_xattn_w_k, L0_xattn_w_v, L0_xattn_w_k_dis, L0_xattn_w_v_dis, L0_xattn_w_gate, L0_xattn_b_gate, L0_xattn_anat_gate_logit, L0_xattn_dis_gate_logit, L0_xattn_w_out, L0_xattn_b_out, L1_xattn_Wq, L1_xattn_Wk, L1_xattn_Wv, L1_xattn_Wq_ca, L1_xattn_Wk_ca, L1_xattn_Wv_ca, L1_xattn_Wout, L1_xattn_b_out):
    import jax
    import jax.numpy as jnp

    def _L0_xattn_ref(hidden_states, encoder_hidden_states, w_q, w_k, w_v, w_k_dis, w_v_dis, w_gate, b_gate, anat_gate_logit, dis_gate_logit, w_out, b_out):
        import jax, jax.numpy as jnp
        import numpy as np
        B, S, D = (32, 128, 160)
        CROSS = 96
        HEADS = 20
        HD = D // HEADS
        N_AOE, N_IMG = (16, 16)
        SCALE = 1.0 / float(np.sqrt(HD))

        def _split_heads(x):
            b, n, _ = x.shape
            return x.reshape(b, n, HEADS, HD).transpose(0, 2, 1, 3)

        def _attend(q, k, v):
            scores = jnp.einsum('bhsd,bhkd->bhsk', q, k) * SCALE
            probs = jax.nn.softmax(scores, axis=-1)
            return jnp.einsum('bhsk,bhkd->bhsd', probs, v)
        residual = hidden_states
        b = hidden_states.shape[0]
        dis_tokens = encoder_hidden_states[:, :N_AOE, :]
        anat_tokens = encoder_hidden_states[:, N_AOE:N_AOE + N_IMG, :]
        query = _split_heads(hidden_states @ w_q.T)
        k_anat = _split_heads(anat_tokens @ w_k.T)
        v_anat = _split_heads(anat_tokens @ w_v.T)
        k_dis = _split_heads(dis_tokens @ w_k_dis.T)
        v_dis = _split_heads(dis_tokens @ w_v_dis.T)
        z_anat = _attend(query, k_anat, v_anat)
        z_dis = _attend(query, k_dis, v_dis)
        severity = dis_tokens.mean(axis=1)
        shift = (severity @ w_gate.T + b_gate).reshape(b, 1, 1, 1)
        anat_gate = jax.nn.sigmoid(anat_gate_logit - shift)
        dis_gate = jax.nn.sigmoid(dis_gate_logit + shift)
        z_final = anat_gate * z_anat + dis_gate * z_dis
        out = z_final.transpose(0, 2, 1, 3).reshape(b, -1, D)
        out = out @ w_out.T + b_out
        out = out + residual
        return out

    def _L1_xattn_ref(hidden_states, encoder_hidden_states, Wq, Wk, Wv, Wq_ca, Wk_ca, Wv_ca, Wout, b_out):
        import jax, jax.numpy as jnp
        import numpy as np
        HEADS = 8
        NUM_TOKENS = 4
        CROSS_ATTENTION_DIM = 96

        def _mha(q, k, v, heads=HEADS):
            B, Sq, H = q.shape
            Sk = k.shape[1]
            d = H // heads
            qh = q.reshape(B, Sq, heads, d).transpose(0, 2, 1, 3)
            kh = k.reshape(B, Sk, heads, d).transpose(0, 2, 1, 3)
            vh = v.reshape(B, Sk, heads, d).transpose(0, 2, 1, 3)
            scores = jnp.einsum('bhqd,bhkd->bhqk', qh, kh) * jnp.asarray(d, q.dtype) ** (-0.5)
            probs = jax.nn.softmax(scores, axis=-1)
            out = jnp.einsum('bhqk,bhkd->bhqd', probs, vh)
            return out.transpose(0, 2, 1, 3).reshape(B, Sq, H)
        residual = hidden_states
        unet_size = residual.shape[1]
        end_pos = encoder_hidden_states.shape[1] - NUM_TOKENS
        enc = encoder_hidden_states[:, :end_pos, :]
        ca = encoder_hidden_states[:, end_pos:, :]
        query = hidden_states @ Wq
        keyt = enc @ Wk
        valt = enc @ Wv
        hs = _mha(query, keyt, valt)
        ca_q1 = jnp.einsum('btc,th->bch', ca, Wq_ca)
        indices = np.linspace(0, CROSS_ATTENTION_DIM - 1, unet_size).astype(np.int64)
        ca_q1 = ca_q1[:, indices, :]
        ca_hs1 = _mha(ca_q1, residual, residual)
        ca_q2 = ca_hs1 @ Wq
        ca_k2 = ca @ Wk_ca
        ca_v2 = ca @ Wv_ca
        ca_hs2 = _mha(ca_q2, ca_k2, ca_v2)
        out = hs + ca_hs2
        out = out @ Wout + b_out
        out = out + residual
        return out
    x = _L0_xattn_ref(x, ctx_768, L0_xattn_w_q, L0_xattn_w_k, L0_xattn_w_v, L0_xattn_w_k_dis, L0_xattn_w_v_dis, L0_xattn_w_gate, L0_xattn_b_gate, L0_xattn_anat_gate_logit, L0_xattn_dis_gate_logit, L0_xattn_w_out, L0_xattn_b_out)
    x = _L1_xattn_ref(x, ctx_768, L1_xattn_Wq, L1_xattn_Wk, L1_xattn_Wv, L1_xattn_Wq_ca, L1_xattn_Wk_ca, L1_xattn_Wv_ca, L1_xattn_Wout, L1_xattn_b_out)
    return x

_drawn_inputs = setup_inputs


def setup_inputs(seed=0):
    import zlib

    import numpy as np

    out = dict(_drawn_inputs(seed))
    spreads = {'L0_xattn_b_out': (0.0, 0.1), 'L1_xattn_b_out': (0.0, 0.1)}
    factors = {'L0_xattn_w_q': 8.0,
     'L0_xattn_w_k': 8.0,
     'L0_xattn_w_v': 4.249,
     'L0_xattn_w_k_dis': 8.0,
     'L0_xattn_w_v_dis': 4.018,
     'L0_xattn_w_gate': 8.0,
     'L0_xattn_w_out': 3.087,
     'L1_xattn_Wq': 8.0,
     'L1_xattn_Wk': 8.0,
     'L1_xattn_Wq_ca': 64.0,
     'L1_xattn_Wk_ca': 23.038}
    for name, (base, spread) in spreads.items():
        noise = np.random.default_rng([zlib.crc32(name.encode()), seed]).standard_normal(out[name].shape)
        drawn = base * np.exp(spread * noise) if base else spread * noise
        out[name] = jnp.asarray(drawn.astype(out[name].dtype))
    for name, factor in factors.items():
        out[name] = (out[name] * factor).astype(out[name].dtype)
    return out
```

```python
import numpy as np

import concourse.bass as bass
from concourse import mybir
from contextlib import ExitStack

B, S, D, C, NKEY, NCA = 8, 256, 160, 96, 1597, 4
NCTX = NKEY + NCA
P = 128
QT = S // P
H0, D0, T0 = 20, 8, 16
HA = P // D0
HB = H0 - HA
H1, D1 = 8, 20
G, HG = 2, 4
PAD = 32
KT = -(-NKEY // P)
LAST = NKEY - (KT - 1) * P
CH = 400
NCH = 4
KW = CH * NCH
NC2 = 96
HALF = 2
UNITS = G * KT * (HG // HALF)
ST = 3
NP = 4
PARTS_K = (0, 0, 0, 1, 1, 2)
PARTS_Q = (0, 1, 2, 0, 1, 0)
TERMS = len(PARTS_K)
KR = TERMS * D1
SPLIT_A = 6 * D1
SPLIT_B = D - SPLIT_A

W128 = dict(ident=128, spread=128, mask_a=HA, mask_b=HB, mask_h=HG, mask_v=64, mask_v4=32, b0p=G,
            b0n=G * P, b1n=D, logits=3, wq0=G * D, wo0a=G * P, wo0b=G * P, wq1=G * 2 * SPLIT_A,
            wqpp=G * G * P, wo1=G * D, mask_v2=G * P)
W96 = dict(wk0=D, wkd0=D, wv0=D, wvd0=D, wg=1, repeat=S, wk1=SPLIT_A + 64, wv1=D, wkca=G * P,
           wvca=G * P, wqca=G * P)


def offsets(table):
    at, out = 0, {}
    for name, n in table.items():
        out[name] = (at, at + n)
        at += n
    return out, at


O128, N128 = offsets(W128)
O96, N96 = offsets(W96)

PREP = ["small", "k0", "q0", "k1", "s0", "k2", "s1", "k3", "s2", "kb0", "kb1", "t0", "t1", "t2",
        "z", "h", "hn", "q1"]
PREP_SLOT = {2 * n: name for n, name in enumerate(PREP)}
RATE_SLOT = {1: "v0", 3: "v1", 5: "v2", 7: "v3", 9: "v4", 11: "ca", 13: "caq", 15: "cs0",
             17: "cs1", 19: "cs2", 21: "cs3", 27: "m0", 31: "ct0", 33: "ct1", 35: "ct2", 37: "ct3",
             39: "c1", 41: "c2", 43: "sc", 47: "pe", 49: "zc", 52: "m1"}
RATE = [RATE_SLOT[n] for n in sorted(RATE_SLOT)]
NRATE, NPREP = len(RATE), len(PREP)
KEYS = ["k0", "k1", "k2", "k3", "kb0", "kb1"]
NMAX = H1 * QT * NCH
PREP_LINKS = 9
RATE_LINKS = 9
KSTORES = 7
KQ_LINKS = 9


class Batch:

    def __init__(self, i, c):
        self.i, self.c, self.par = i, c, c % 2

    @property
    def n(self):
        return 2 * self.i + self.c

    @property
    def half(self):
        return self.i + self.c // 2


def wait(eng, sem, value):
    if not (isinstance(value, int) and value <= 0):
        eng.wait_ge(sem, value)


def steps(eng, step):
    one = lambda c: Batch(0, c)
    step(one(0), None, None, None)
    step(one(1), one(0), None, None)
    step(one(2), one(1), one(0), None)
    with eng.Fori(0, 2) as i:
        for c in (1, 2):
            step(Batch(i, c + 2), Batch(i, c + 1), Batch(i, c), Batch(i, c - 1))
    step(one(7), one(6), one(5), one(4))
    step(None, one(7), one(6), one(5))
    step(None, None, one(7), one(6))
    step(None, None, None, one(7))


def program(nc, x_t, x_n, ctx_t, ca_n, w128, w96, out):
    fp32, bf16 = mybir.dt.float32, mybir.dt.bfloat16
    ALU, ACT, AX = mybir.AluOpType, mybir.ActivationFunctionType, mybir.AxisListType
    SC0 = 1.0 / float(np.sqrt(D0))
    SC1 = float(D1) ** -0.5

    ctx = ExitStack()
    with ctx:
        def sb(name, shape, dt=fp32):
            return ctx.enter_context(nc.sbuf_tensor(name, shape, dt))

        def sem(name):
            return ctx.enter_context(nc.semaphore(name))

        wp = sb("wp", [P, N128])
        wc = sb("wc", [C, N96])

        def W(name, rows=P):
            return wp[0:rows, O128[name][0]:O128[name][1]]

        def Wc(name, rows=C):
            return wc[0:rows, O96[name][0]:O96[name][1]]

        cT = [sb(f"cT{p}", [C, NCTX]) for p in range(2)]
        can = [sb(f"can{p}", [NCA, C]) for p in range(2)]
        sev = sb("sev", [C, 1])
        tok0 = sb("tok0", [C, 2, 8, T0])
        tok2 = sb("tok2", [C, H1, NCA])
        gz = sb("gz", [P, 2])
        gate = sb("gate", [P, 2])
        kb0a = sb("kb0a", [P, 2, HA, T0])
        kb0b = sb("kb0b", [HB * D0, 2, HB, T0])
        vb0 = sb("vb0", [P, 4, 64])
        vb4 = sb("vb4", [P, 32])
        q0a = sb("q0a", [P, S])
        q0b = sb("q0b", [HB * D0, S])
        e0 = sb("e0", [P, QT, 2 * H0 * T0])
        m0x = sb("m0x", [P, QT, 2 * H0])
        d0 = sb("d0", [P, QT, 2 * H0])
        pT0 = sb("pT0", [P, 5, S])
        z0a = sb("z0a", [P, S])
        z0b = sb("z0b", [HB * D0, S])
        hT = [sb(f"hT{p}", [P, G, S]) for p in range(2)]
        hn = [sb(f"hn{p}", [P, QT, G * P]) for p in range(2)]
        res = [sb(f"res{p}", [P, QT, D]) for p in range(2)]
        qs = e0[0:SPLIT_A, 0, 0:2 * S]
        qsp = sb("qsp", [SPLIT_A, 3, 2 * S], bf16)
        kr = sb("kr", [P, 2, CH])
        qr = kr[0:SPLIT_A, :, :].rearrange("p a n -> p (a n)")[:, 0:2 * S]
        kspa = sb("kspa", [SPLIT_A, 3, KW], bf16)
        kspb = sb("kspb", [P, 3, 2, CH], bf16)
        ka = [sb(f"ka{p}", [KR + 3, H1, KW], bf16) for p in range(2)]
        qa = [sb(f"qa{p}", [KR + 3, H1, S], bf16) for p in range(2)]
        mx = sb("mx", [P, H1 * QT, NCH])
        nm = sb("nm", [P, H1 * QT])
        mr = sb("mr", [HG * QT, P])
        msp = sb("msp", [HG * QT, 3, P], bf16)
        v = [sb(f"v{p}", [P, KT, H1, PAD]) for p in range(2)]
        pr = sb("pr", [P, NP, HALF * S])
        k2b = sb("k2b", [P, G, HG, NCA])
        v2b = sb("v2b", [H1 * NCA, G * P])
        caq = sb("caq", [P, G, NC2])
        caqb = sb("caqb", [P, G, HG, NC2])
        cm = sb("cm", [NC2, H1])
        cden = sb("cden", [NC2, H1])
        pc = sb("pc", [NC2, H1, S])
        pcT = sb("pcT", [P, H1, QT, NC2])
        c1T = sb("c1T", [P, G, NC2])
        c2T = sb("c2T", [P, G, NC2])
        p2 = sb("p2", [NC2, H1, NCA])
        m2 = sb("m2", [NC2, H1])
        d2 = sb("d2", [NC2, H1])
        p2e = sb("p2e", [H1 * NCA, S])
        zc = [sb(f"zc{p}", [P, G, S]) for p in range(2)]
        us = sb("us", [P, G, S])
        rb = sb("rb", [P, G, S])
        o1 = rb[:, :, :].rearrange("p g s -> p (g s)")[:, 0:QT * D]

        bank = [ctx.enter_context(nc.psum_tensor(f"bank{n}", [P, 512], fp32)) for n in range(8)]
        U, SX, M0, M1 = bank[3], bank[4:6], bank[6], bank[7]

        kscr = nc.dram_tensor("kscr", (2, 3, D, KW), bf16).ap()
        qscr = nc.dram_tensor("qscr", (2, 3, D, S), bf16).ap()
        mscr = nc.dram_tensor("mscr", (G, 3, HG * QT, P), bf16).ap()

        w_loaded = sem("w_loaded")
        in_loaded = [sem(f"in_loaded{p}") for p in range(2)]
        ones_loaded = sem("ones_loaded")
        consts = sem("consts")
        m0_full, m0_read = sem("m0_full"), sem("m0_read")
        m1_full, m1_read = sem("m1_full"), sem("m1_read")
        fin_full, fin_read = sem("fin_full"), sem("fin_read")
        sev_ready = sem("sev_ready")
        gz_ready, gz_exp = sem("gz_ready"), sem("gz_exp")
        prep_chain = sem("prep_chain")
        rate_chain = sem("rate_chain")
        split_chain = sem("split_chain")
        z_chain = sem("z_chain")
        e0_exp, w0_ready, p0_ready = sem("e0_exp"), sem("w0_ready"), sem("p0_ready")
        tok0_ready, tok2_ready = sem("tok0_ready"), sem("tok2_ready")
        xb_ready = sem("xb_ready")
        k1_ready = sem("k1_ready")
        ksp_ready, qsp_ready = sem("ksp_ready"), sem("qsp_ready")
        kscr_done, qscr_done = sem("kscr_done"), sem("qscr_done")
        kq_loaded = [[sem(f"kq_loaded{p}{g}") for g in range(G)] for p in range(2)]
        sx_full, sx_read = sem("sx_full"), sem("sx_read")
        msp_ready = sem("msp_ready")
        mscr_done = sem("mscr_done")
        m_loaded = [sem(f"m_loaded{g}") for g in range(G)]
        st_full, exp_done, pv_done = sem("st_full"), sem("exp_done"), sem("pv_done")
        caqb_ready, cm_ready = sem("caqb_ready"), sem("cm_ready")
        cden_ready, pc_ready = sem("cden_ready"), sem("pc_ready")
        s2_exp, p2_ready = sem("s2_exp"), sem("p2_ready")
        res_ready = sem("res_ready")
        u_read, z1_ready = sem("u_read"), sem("z1_ready")
        out_stored = sem("out_stored")
        passed = sem("passed")

        prep_no = lambda b, name: NPREP * b.n + PREP.index(name) + 1
        rate_no = lambda b, name: NRATE * b.n + RATE.index(name) + 1

        def chunks_of(k):
            return [(n // (QT * NCH), n // NCH % QT, n % NCH, n)
                    for n in range(k * NMAX // UNITS, (k + 1) * NMAX // UNITS)]

        def unit(k):
            return k // (KT * 2), k // 2 % KT, k % 2

        def st_bank(b, k):
            return bank[(k + b.par) % ST]

        def last_use(b, k):
            if k >= ST:
                return k - ST
            return next(n for n in (-1, -2, -3) if (UNITS + n + 1 - b.par) % ST == (k + b.par) % ST)

        def on_its_own(eng):
            eng.sem_inc(passed, 1)

        block = ctx.enter_context(nc.Block())

        @block.sync
        def _(sp):
            sp.dma_start(wc[:, :], w96).then_inc(w_loaded, 16)
            sp.dma_start(wp[:, :], w128).then_inc(w_loaded, 16)
            sp.wait_ge(consts, 1)
            for p in range(2):
                sp.dma_start(ka[p][KR:KR + 3, :, :], kspa[0:3, 0:1, :].broadcast_to([3, H1, KW]))\
                  .then_inc(ones_loaded, 16)

            def load_parts(b, g):
                sp.wait_ge(kscr_done, 16 * KSTORES * (b.n + 1))
                on_its_own(sp)
                sp.wait_ge(qscr_done, 16 * 2 * (b.n + 1))
                on_its_own(sp)
                wait(sp, st_full, UNITS * (b.n - 2) + (g + 1) * (UNITS // G))
                on_its_own(sp)
                for t in range(TERMS):
                    for stack, scr, parts in ((ka, kscr, PARTS_K), (qa, qscr, PARTS_Q)):
                        src = scr[b.par, parts[t]].rearrange("(g h d) n -> g d h n", g=G, h=HG)[g]
                        sp.dma_start(stack[b.par][t * D1:(t + 1) * D1, g * HG:(g + 1) * HG, :], src)\
                          .then_inc(kq_loaded[b.par][g], 16)

            def step(prep, rate, att, fin):
                if prep:
                    p = prep.par
                    wait(sp, m1_full, NRATE * (prep.n - 2) + RATE.index("c1") + 1)
                    on_its_own(sp)
                    wait(sp, res_ready, prep.n - 1)
                    on_its_own(sp)
                    sp.dma_start(cT[p][:, :], ctx_t[bass.ds(prep.n, 1)].rearrange("a c n -> (a c) n")).then_inc(in_loaded[p], 16)
                    sp.dma_start(hT[p][:, :, :], x_t[bass.ds(prep.n, 1)].rearrange("a p g s -> (a p) g s")).then_inc(in_loaded[p], 16)
                    sp.dma_start(hn[p][:, :, :], x_n[bass.ds(prep.n, 1)].rearrange("a p q d -> (a p) q d")).then_inc(in_loaded[p], 16)
                    sp.dma_start(can[p][:, :], ca_n[bass.ds(prep.n, 1)].rearrange("a t c -> (a t) c")).then_inc(in_loaded[p], 16)
                if rate:
                    load_parts(rate, 1)
                if fin:
                    sp.wait_ge(fin_read, 3 * (fin.n + 1))
                    on_its_own(sp)
                    sp.dma_start(out[bass.ds(fin.n, 1)].rearrange("a (t q) d -> q (a t) d", q=P), o1.rearrange("p (t d) -> p t d", t=QT))\
                      .then_inc(out_stored, 16)
                if prep:
                    wait(sp, kq_loaded[prep.par][1], 16 * 2 * TERMS * prep.half)
                    on_its_own(sp)
                    sp.wait_ge(ksp_ready, 6 * (prep.n + 1))
                    on_its_own(sp)
                    dst = kscr[prep.par].rearrange("a r n -> r a n")
                    sp.dma_start(dst[0:SPLIT_A], kspa[:, :, :]).then_inc(kscr_done, 16)
                    for u in range(2):
                        for a in range(3):
                            sp.dma_start(kscr[prep.par, a, SPLIT_A:D].rearrange("r (c u n) -> u r c n", c=2, u=2)[u],
                                         kspb[64 * u:64 * u + SPLIT_B, a, :, :]).then_inc(kscr_done, 16)
                    sp.wait_ge(qsp_ready, prep.n + 1)
                    on_its_own(sp)
                    dst = qscr[prep.par].rearrange("a r n -> r a n")
                    sp.dma_start(dst[0:SPLIT_A], qsp[:, :, 0:S]).then_inc(qscr_done, 16)
                    sp.dma_start(dst[SPLIT_A:D], qsp[0:SPLIT_B, :, S:2 * S]).then_inc(qscr_done, 16)
                    load_parts(prep, 0)

            steps(sp, step)
            sp.wait_ge(out_stored, 16 * B)

        @block.tensor
        def _(pe):
            def mm(o, lhs, rhs, start=True, stop=True):
                return nc.tensor.matmul(o, lhs, rhs, start=start, stop=stop)

            pe.wait_ge(w_loaded, 32)
            pe.wait_ge(consts, 3)
            pe.wait_ge(ones_loaded, 32)
            tok = [slice(T0, 2 * T0), slice(0, T0)]
            tail = slice(NKEY, NCTX)

            def prep_piece(b, name):
                p, at = b.par, PREP.index(name)
                wait(pe, m0_read, NPREP * b.n + at)
                wk = [Wc("wk0"), Wc("wkd0")]
                wv = [Wc("wv0"), Wc("wvd0")]
                if name == "small":
                    pe.wait_ge(in_loaded[p], 64 * (b.half + 1))
                    pe.wait_ge(tok0_ready, b.n + 1)
                    for s in range(2):
                        r8 = tok0[:, s, :, :].rearrange("p h k -> p (h k)")
                        t = cT[p][:, tok[s]]
                        mm(M0[:, s * T0:(s + 1) * T0], wk[s][:, 0:P], t)
                        mm(M0[0:HB * D0, 32 + s * T0:32 + (s + 1) * T0], wk[s][:, P:D], t)
                        for u in range(2):
                            c = 2 * s + u
                            mm(M0[:, 64 + 64 * c:128 + 64 * c],
                               r8, wv[s][:, 64 * u:64 * u + 64])
                        mm(M0[64 * s:64 * s + 64, 320:352],
                           r8[:, 0:HB * T0], wv[s][:, P:D])
                    pe.wait_ge(sev_ready, b.n + 1)
                    last = mm(M0[:, 352:353], Wc("wg").broadcast_to([C, P]), sev[:, :])
                elif name == "q0":
                    for cols, o in ((slice(0, P), M0[:, 0:S]), (slice(P, D), M0[0:HB * D0, S:2 * S])):
                        for g in range(G):
                            last = mm(o, W("wq0").rearrange("p (g d) -> p g d", g=G)[:, g, cols],
                                      hT[p][:, g, :], g == 0, g == G - 1)
                elif name in ("k0", "k1", "k2", "k3"):
                    c = int(name[1])
                    last = mm(M0[0:SPLIT_A, 0:CH], Wc("wk1")[:, 0:SPLIT_A], cT[p][:, c * CH:(c + 1) * CH])
                elif name in ("kb0", "kb1"):
                    for u in range(2):
                        c = 2 * int(name[2]) + u
                        last = mm(M0[64 * u:64 * u + 64, 0:CH], Wc("wk1")[:, SPLIT_A:SPLIT_A + 64],
                                  cT[p][:, c * CH:(c + 1) * CH])
                elif name in ("s0", "s1"):
                    t = int(name[1])
                    last = mm(M0[:, :], q0a[:, t * P:(t + 1) * P], kb0a[:, :, :, :].rearrange("p s h k -> p (s h k)"))
                elif name == "s2":
                    for t in range(QT):
                        last = mm(M0[:, t * P:(t + 1) * P], q0b[:, t * P:(t + 1) * P],
                                  kb0b[:, :, :, :].rearrange("p s h k -> p (s h k)"))
                elif name in ("t0", "t1", "t2"):
                    pe.wait_ge(p0_ready, b.n + 1)
                    for c in range(2 * int(name[1]), min(2 * int(name[1]) + 2, 5)):
                        for t in range(QT):
                            o = (c % 2) * S + t * P
                            last = nc.tensor.transpose(M0[:, o:o + P], e0[:, t, c * P:(c + 1) * P], W("ident"))
                elif name == "z":
                    for u in range(2):
                        for s in range(2):
                            mm(M0[64 * u:64 * u + 64, 0:S], vb0[:, 2 * s + u, :], pT0[:, 2 * s + u, :],
                               s == 0, s == 1)
                    last = mm(M0[0:32, S:2 * S], vb4[:, :], pT0[:, 4, :])
                elif name == "h":
                    for g in range(G):
                        o = M0[:, g * S:(g + 1) * S]
                        mm(o, W("wo0a")[:, g * P:(g + 1) * P], z0a[:, :], True, False)
                        last = mm(o, W("wo0b", 32)[:, g * P:(g + 1) * P], z0b[:, :], False, True)
                elif name == "hn":
                    for t in range(QT):
                        o = M0[:, t * G * P:(t + 1) * G * P]
                        mm(o, z0a[:, t * P:(t + 1) * P], W("wo0a"), True, False)
                        last = mm(o, z0b[:, t * P:(t + 1) * P], W("wo0b", 32), False, True)
                elif name == "q1":
                    w = W("wq1").rearrange("p (g d) -> p g d", g=G)
                    for u in range(2):
                        for g in range(G):
                            last = mm(M0[0:SPLIT_A, u * S:(u + 1) * S], w[:, g, u * SPLIT_A:(u + 1) * SPLIT_A],
                                      hT[p][:, g, :], g == 0, g == G - 1)
                last.then_inc(m0_full, 1)

            def rate_piece(b, name):
                p, at = b.par, RATE.index(name)
                wait(pe, m1_read, NRATE * b.n + at)
                if name[0] == "v":
                    for t in range(3 * int(name[1]), min(3 * int(name[1]) + 3, KT)):
                        rows = P if t < KT - 1 else LAST
                        o = (t % 3) * D
                        last = mm(M1[0:rows, o:o + D], cT[p][:, t * P:t * P + rows], Wc("wv1"))
                elif name == "ca":
                    for g in range(G):
                        mm(M1[:, g * NCA:(g + 1) * NCA], Wc("wkca")[:, g * P:(g + 1) * P], cT[p][:, tail])
                    pe.wait_ge(tok2_ready, b.n + 1)
                    last = mm(M1[0:H1 * NCA, S:2 * S], tok2[:, :, :].rearrange("p h k -> p (h k)"),
                              Wc("wvca"))
                elif name == "caq":
                    for g in range(G):
                        last = mm(M1[:, g * NC2:(g + 1) * NC2], Wc("wqca", NCA)[:, g * P:(g + 1) * P],
                                  can[p][:, :])
                elif name[:2] == "cs":
                    pe.wait_ge(caqb_ready, b.n + 1)
                    for u in range(2):
                        h = 2 * int(name[2]) + u
                        last = mm(M1[0:NC2, u * S:(u + 1) * S], caqb[:, h // HG, h % HG, :],
                                  hT[p][:, h // HG, :])
                elif name[:2] == "ct":
                    pe.wait_ge(pc_ready, b.n + 1)
                    for n in range(4):
                        h, t = 2 * int(name[2]) + n // 2, n % 2
                        last = nc.tensor.transpose(M1[:, n * NC2:(n + 1) * NC2], pc[:, h, t * P:(t + 1) * P],
                                                   W("ident", NC2)[:, 0:NC2])
                elif name == "c1":
                    for g in range(G):
                        for t in range(QT):
                            for j in range(HG):
                                last = mm(M1[PAD * j:PAD * (j + 1), g * NC2:(g + 1) * NC2],
                                          hn[p][:, t, g * P + PAD * j:g * P + PAD * (j + 1)],
                                          pcT[:, g * HG + j, t, :], t == 0, t == QT - 1)
                elif name == "c2":
                    w = W("wqpp").rearrange("p (a g d) -> p a g d", a=G, g=G)
                    for g in range(G):
                        for a in range(G):
                            last = mm(M1[:, g * NC2:(g + 1) * NC2], w[:, a, g, :], c1T[:, a, :],
                                      a == 0, a == G - 1)
                elif name == "sc":
                    for g in range(G):
                        last = mm(M1[0:NC2, g * HG * NCA:(g + 1) * HG * NCA], c2T[:, g, :],
                                  k2b[:, g, :, :].rearrange("p h t -> p (h t)"))
                elif name == "pe":
                    pe.wait_ge(p2_ready, b.n + 1)
                    last = mm(M1[0:H1 * NCA, 0:S], p2[:, :, :].rearrange("p h t -> p (h t)"),
                              Wc("repeat", NC2))
                elif name == "zc":
                    for g in range(G):
                        last = mm(M1[:, g * S:(g + 1) * S], v2b[:, g * P:(g + 1) * P], p2e[:, :])
                else:
                    g = int(name[1])
                    pe.wait_ge(rate_chain, RATE_LINKS * b.n + (1, 7)[g])
                    n = HG * QT
                    last = nc.tensor.transpose(M1[0:n, 0:P], nm[:, g * n:(g + 1) * n], W("ident"))
                last.then_inc(m1_full, 1)

            def max_scores(b, k):
                p = b.par
                for h, t, c, n in chunks_of(k):
                    if n % (HG * QT * NCH) == 0:
                        pe.wait_ge(kq_loaded[p][h // HG], 16 * 2 * TERMS * (b.half + 1))
                    wait(pe, sx_read, NMAX * b.n + n - 1)
                    w = min(CH, NKEY - c * CH)
                    mm(SX[n % 2][:, 0:w], qa[p][0:KR, h, t * P:(t + 1) * P], ka[p][0:KR, h, c * CH:c * CH + w])\
                        .then_inc(sx_full, 1)

            def scores(b, k):
                p = b.par
                g, t, u = unit(k)
                if k % (UNITS // G) == 0:
                    pe.wait_ge(m_loaded[g], 16 * (b.n + 1))
                wait(pe, exp_done, UNITS * b.n + last_use(b, k) + 1)
                rows = P if t < KT - 1 else LAST
                for j in range(HALF):
                    h = g * HG + HALF * u + j
                    last = mm(st_bank(b, k)[0:rows, j * S:(j + 1) * S], ka[p][:, h, t * P:t * P + rows],
                              qa[p][:, h, :])
                last.then_inc(st_full, 1)

            def values(b, k):
                p = b.par
                g, t, u = unit(k)
                if k % (UNITS // G) == 0:
                    if g == 0:
                        pe.wait_ge(m1_read, rate_no(b, "v4"))
                    wait(pe, u_read, G * b.n + g)
                pe.wait_ge(exp_done, UNITS * b.n + k + 1)
                rows = P if t < KT - 1 else LAST
                if rows < P:
                    on_its_own(pe)
                for j in range(HALF):
                    q = HALF * u + j
                    last = mm(U[PAD * q:PAD * (q + 1), g * S:(g + 1) * S], v[p][0:rows, t, g * HG + q, :],
                              pr[0:rows, k % NP, j * S:(j + 1) * S], t == 0, t == KT - 1)
                last.then_inc(pv_done, 1)

            def denominators(b, g):
                pe.wait_ge(u_read, G * b.n + g + 1)
                wait(pe, fin_read, 3 * b.n + g)
                mm(M1[:, 0:S], W("spread"), us[:, g, :]).then_inc(fin_full, 1)

            def project(b):
                pe.wait_ge(z1_ready, G * (b.n + 1))
                pe.wait_ge(fin_read, 3 * b.n + 2)
                for t in range(QT):
                    for g in range(G):
                        last = mm(M1[:, t * D:(t + 1) * D], us[:, g, t * P:(t + 1) * P],
                                  W("wo1").rearrange("p (g d) -> p g d", g=G)[:, g, :], g == 0, g == G - 1)
                last.then_inc(fin_full, 1)

            def step(prep, rate, att, fin):
                for k in range(UNITS):
                    if att:
                        scores(att, k)
                        if k:
                            values(att, k - 1)
                    if rate:
                        max_scores(rate, k)
                    if prep and k in PREP_SLOT:
                        prep_piece(prep, PREP_SLOT[k])
                    if rate and k in RATE_SLOT:
                        if k in (5, 9) and fin:
                            pe.wait_ge(fin_read, 3 * fin.n + (2 if k == 5 else 3))
                        if k == 31 and att:
                            pe.wait_ge(fin_read, 3 * att.n + 1)
                        rate_piece(rate, RATE_SLOT[k])
                    if k == 3 and fin:
                        pe.wait_ge(m1_read, rate_no(rate, "v1") if rate else NRATE * B)
                        denominators(fin, 1)
                    if k == 7 and fin:
                        pe.wait_ge(m1_read, rate_no(rate, "v3") if rate else NRATE * B)
                        project(fin)
                    if k == 29 and att:
                        pe.wait_ge(m1_read, rate_no(rate, "m0") if rate else NRATE * B)
                        denominators(att, 0)
                if att:
                    values(att, UNITS - 1)
                if rate:
                    rate_piece(rate, "m1")

            steps(pe, step)

        @block.scalar
        def _(act):
            def f(o, i, func=ACT.Copy, **kw):
                return nc.scalar.activation(o, i, func, **kw)

            def prep_piece(b, name):
                if name in ("k0", "k1", "k2", "k3", "kb0", "kb1"):
                    act.wait_ge(m0_full, prep_no(b, name))
                    wait(act, kscr_done, 16 * KSTORES * b.n)
                    n = int(name[-1])
                    if len(name) == 2:
                        f(kspa[:, 0, n * CH:(n + 1) * CH], M0[0:SPLIT_A, 0:CH]).then_inc(k1_ready, 1)
                    else:
                        f(kspb[:, 0, n, :], M0[:, 0:CH]).then_inc(k1_ready, 1)
                elif name == "q0":
                    act.wait_ge(m0_full, prep_no(b, name))
                    f(q0a[:, :], M0[:, 0:S], scale=SC0)
                    f(q0b[:, :], M0[0:HB * D0, S:2 * S], scale=SC0).then_inc(m0_read, 1)
                elif name in ("t0", "t1", "t2"):
                    act.wait_ge(m0_full, prep_no(b, name))
                    n = int(name[1])
                    w = 1 if n == 2 else 2
                    f(pT0[:, 2 * n:2 * n + w, :].rearrange("p a s -> p (a s)"), M0[:, 0:w * S]).then_inc(m0_read, 1)
                elif name == "z":
                    act.wait_ge(m0_full, prep_no(b, name))
                    f(z0a[:, :], M0[:, 0:S])
                    f(z0b[:, :], M0[0:32, S:2 * S]).then_inc(m0_read, 1)
                elif name == "q1":
                    act.wait_ge(m0_full, prep_no(b, name))
                    wait(act, qsp_ready, b.n)
                    f(qs, M0[0:SPLIT_A, :], scale=SC1).then_inc(m0_read, 1)

            def rate_piece(b, name):
                p = b.par
                if name[0] == "v":
                    act.wait_ge(m1_full, rate_no(b, name))
                    wait(act, pv_done, UNITS * (b.n - 1))
                    n = int(name[1])
                    t0, t1 = 3 * n, min(3 * n + 3, KT)
                    rows = P if t1 < KT else LAST
                    f(v[p][0:rows, t0:t1, :, 0:D1],
                      M1[0:rows, 0:(t1 - t0) * D].rearrange("p (t h d) -> p t h d", h=H1, d=D1))\
                        .then_inc(m1_read, 1)
                elif name == "caq":
                    act.wait_ge(m1_full, rate_no(b, name))
                    wait(act, caqb_ready, b.n)
                    f(caq[:, :, :].rearrange("p g c -> p (g c)"), M1[:, 0:G * NC2], scale=SC1).then_inc(m1_read, 1)
                elif name[:2] == "cs":
                    n = int(name[2])
                    act.wait_ge(cm_ready, 4 * b.n + n + 1)
                    for u in range(2):
                        h = 2 * n + u
                        last = f(pc[:, h, :], M1[0:NC2, u * S:(u + 1) * S], ACT.Exp, bias=cm[:, h:h + 1],
                                 accum_out=cden[:, h:h + 1])
                    last.then_inc(m1_read, 1)
                elif name[:2] == "ct":
                    act.wait_ge(m1_full, rate_no(b, name))
                    n = int(name[2])
                    f(pcT[:, 2 * n:2 * n + 2, :, :].rearrange("p h t c -> p (h t c)"), M1[:, 0:4 * NC2]).then_inc(m1_read, 1)
                elif name == "c1":
                    act.wait_ge(m1_full, rate_no(b, name))
                    f(c1T[:, :, :].rearrange("p g c -> p (g c)"), M1[:, 0:G * NC2]).then_inc(m1_read, 1)
                elif name == "c2":
                    act.wait_ge(m1_full, rate_no(b, name))
                    f(c2T[:, :, :].rearrange("p g c -> p (g c)"), M1[:, 0:G * NC2], scale=SC1).then_inc(m1_read, 1)
                elif name == "pe":
                    act.wait_ge(m1_full, rate_no(b, name))
                    f(p2e[:, :], M1[0:H1 * NCA, 0:S]).then_inc(m1_read, 1)
                elif name == "zc":
                    act.wait_ge(m1_full, rate_no(b, name))
                    wait(act, z1_ready, G * (b.n - 1))
                    f(zc[p][:, :, :].rearrange("p g s -> p (g s)"), M1[:, :]).then_inc(m1_read, 1)

            def copy_u(b, g):
                act.wait_ge(pv_done, UNITS * b.n + (g + 1) * (UNITS // G))
                wait(act, fin_full, 3 * b.n)
                f(us[:, g, :], U[:, g * S:(g + 1) * S]).then_inc(u_read, 1)

            def step(prep, rate, att, fin):
                for k in range(UNITS + 1):
                    if k == 0 and fin:
                        copy_u(fin, 1)
                    if att and k < UNITS:
                        act.wait_ge(st_full, UNITS * att.n + k + 1)
                        wait(act, pv_done, UNITS * att.n + k - NP + 1)
                        g, t, u = unit(k)
                        rows = P if t < KT - 1 else LAST
                        f(pr[0:rows, k % NP, :], st_bank(att, k)[0:rows, :], ACT.Exp).then_inc(exp_done, 1)
                    if prep and k in PREP_SLOT:
                        prep_piece(prep, PREP_SLOT[k])
                    if prep and k == 3:
                        act.wait_ge(gz_ready, prep.n + 1)
                        f(gate[:, :], gz[:, :], ACT.Exp).then_inc(gz_exp, 1)
                    if prep and PREP_SLOT.get(k) == "s2":
                        act.wait_ge(m0_read, prep_no(prep, "s2"))
                        f(e0[:, :, :].rearrange("p t n -> p (t n)"), e0[:, :, :].rearrange("p t n -> p (t n)"),
                          ACT.Exp).then_inc(e0_exp, 1)
                    if rate and k in RATE_SLOT:
                        rate_piece(rate, RATE_SLOT[k])
                    if rate and k == 44:
                        act.wait_ge(m1_read, rate_no(rate, "sc"))
                        f(p2[:, :, :].rearrange("p h t -> p (h t)"), p2[:, :, :].rearrange("p h t -> p (h t)"),
                          ACT.Exp).then_inc(s2_exp, 1)
                    if k == 27 and att:
                        copy_u(att, 0)

            act.wait_ge(ones_loaded, 32)
            steps(act, step)

        @block.vector
        def _(dve):
            dve.wait_ge(w_loaded, 32)
            mult, add, sub = ALU.mult, ALU.add, ALU.subtract

            def tt(o, a, b, op):
                return nc.vector.tensor_tensor(o, a, b, op)

            def prep_piece(b, name):
                p = b.par
                full = lambda: dve.wait_ge(m0_full, prep_no(b, name))
                if name == "small":
                    full()
                    lg = W("logits")
                    at = PREP_LINKS * b.n
                    nc.vector.tensor_scalar(gz[:, 0:1], M0[:, 352:353], 1.0 / T0, lg[:, 0:1], mult, add)\
                        .then_inc(prep_chain, 1)
                    dve.wait_ge(prep_chain, at + 1)
                    nc.vector.tensor_scalar(gz[:, 1:2], gz[:, 0:1], -1.0, lg[:, 2:3], mult, sub)\
                        .then_inc(prep_chain, 1)
                    dve.wait_ge(prep_chain, at + 2)
                    tt(gz[:, 0:1], gz[:, 0:1], lg[:, 1:2], sub).then_inc(gz_ready, 1)
                    for s in range(2):
                        tt(kb0a[:, s], M0[:, s * T0:(s + 1) * T0].unsqueeze(1).broadcast_to([P, HA, T0]),
                           W("mask_a").unsqueeze(2).broadcast_to([P, HA, T0]), mult)
                        tt(kb0b[:, s],
                           M0[0:32, 32 + s * T0:32 + (s + 1) * T0].unsqueeze(1).broadcast_to([32, HB, T0]),
                           W("mask_b", 32).unsqueeze(2).broadcast_to([32, HB, T0]), mult)
                    tt(vb0[:, :, :], M0[:, 64:320].rearrange("p (c n) -> p c n", c=4),
                       W("mask_v").unsqueeze(1).broadcast_to([P, 4, 64]), mult)
                    tt(vb4[:, :], M0[:, 320:352], W("mask_v4"), mult).then_inc(m0_read, 1)
                elif name[0] == "k":
                    full()
                    n = int(name[-1])
                    at = KEYS.index(name)
                    dve.wait_ge(k1_ready, len(KEYS) * b.n + at + 1)
                    wait(dve, ksp_ready, len(KEYS) * b.n + at - 1)
                    wait(dve, qsp_ready, b.n)
                    first = kspa[:, 0, n * CH:(n + 1) * CH] if len(name) == 2 else kspb[:, 0, n, :]
                    rows = SPLIT_A if len(name) == 2 else P
                    tt(kr[0:rows, at % 2, :], M0[0:rows, 0:CH], first, sub).then_inc(m0_read, 1)
                elif name in ("s0", "s1", "s2"):
                    full()
                    wait(dve, qsp_ready, b.n)
                    n = int(name[1])
                    wait(dve, m0_read, NPREP * (b.n - 1) + PREP.index("t2") + 1)
                    if n < 2:
                        src = M0[:, :].rearrange("p (g k) -> p g k", k=T0)
                        dst = e0[:, n, 0:512].rearrange("p (g k) -> p g k", k=T0)
                        m = m0x[:, n, 0:2 * HA]
                        mb = m.unsqueeze(2).broadcast_to([P, 2 * HA, T0])
                    else:
                        src = M0[:, 0:256].rearrange("p (t g k) -> p t g k", t=QT, k=T0)
                        dst = e0[:, :, 512:640].rearrange("p t (g k) -> p t g k", k=T0)
                        m = m0x[:, :, 2 * HA:2 * H0]
                        mb = m.unsqueeze(3).broadcast_to([P, QT, 2 * HB, T0])
                    nc.vector.reduce_max(m, src, AX.X).then_inc(prep_chain, 1)
                    dve.wait_ge(prep_chain, PREP_LINKS * b.n + 5 + n)
                    tt(dst, src, mb, sub).then_inc(m0_read, 1)
                elif name == "h":
                    full()
                    for g in range(G):
                        last = nc.vector.scalar_tensor_tensor(out=hT[p][:, g, :], in0=M0[:, g * S:(g + 1) * S],
                                                              scalar=W("b0p")[:, g:g + 1], in1=hT[p][:, g, :],
                                                              op0=add, op1=add)
                    last.then_inc(m0_read, 1)
                elif name == "hn":
                    full()
                    dve.wait_ge(xb_ready, b.n + 1)
                    tt(hn[p][:, :, :].rearrange("p t d -> p (t d)"), M0[:, :],
                       hn[p][:, :, :].rearrange("p t d -> p (t d)"), add).then_inc(m0_read, 1)

            def rate_piece(b, name):
                p = b.par
                full = lambda: dve.wait_ge(m1_full, rate_no(b, name))
                base = RATE_LINKS * b.n
                if name == "ca":
                    full()
                    for g in range(G):
                        tt(k2b[:, g], M1[:, g * NCA:(g + 1) * NCA].unsqueeze(1).broadcast_to([P, HG, NCA]),
                           W("mask_h").unsqueeze(2).broadcast_to([P, HG, NCA]), mult)
                    tt(v2b[:, :], M1[0:H1 * NCA, S:2 * S], W("mask_v2", H1 * NCA), mult).then_inc(m1_read, 1)
                elif name[:2] == "cs":
                    full()
                    n = int(name[2])
                    nc.vector.tensor_reduce(cm[:, 2 * n:2 * n + 2], M1[0:NC2, :].rearrange("p (h s) -> p h s", h=2),
                                            AX.X, ALU.max, negate=True).then_inc(cm_ready, 1)
                elif name == "sc":
                    full()
                    s = M1[0:NC2, 0:H1 * NCA].rearrange("p (h t) -> p h t", h=H1)
                    nc.vector.reduce_max(m2[:, :], s, AX.X).then_inc(rate_chain, 1)
                    dve.wait_ge(rate_chain, base + 4)
                    tt(p2[:, :, :], s, m2[:, :].unsqueeze(2).broadcast_to([NC2, H1, NCA]), sub).then_inc(m1_read, 1)
                elif name in ("m0", "m1"):
                    g = int(name[1])
                    full()
                    wait(dve, mscr_done, 16 * (G * b.n + g))
                    at = base + (1, 7)[g]
                    m = M1[0:HG * QT, 0:P]
                    nc.vector.tensor_copy(msp[:, 0, :], m).then_inc(rate_chain, 1)
                    dve.wait_ge(rate_chain, at + 1)
                    tt(mr[:, :], m, msp[:, 0, :], sub).then_inc(m1_read, 1)
                    dve.wait_ge(m1_read, rate_no(b, name))
                    nc.vector.tensor_copy(msp[:, 1, :], mr[:, :]).then_inc(rate_chain, 1)
                    dve.wait_ge(rate_chain, at + 2)
                    tt(msp[:, 2, :], mr[:, :], msp[:, 1, :], sub).then_inc(msp_ready, 1)

            def group_max(b, g):
                n = HG * QT
                dve.wait_ge(sx_read, NMAX * b.n + (g + 1) * n * NCH)
                nc.vector.tensor_reduce(nm[:, g * n:(g + 1) * n], mx[:, g * n:(g + 1) * n, :], AX.X, ALU.max,
                                        negate=True).then_inc(rate_chain, 1)

            def step(prep, rate, att, fin):
                for k in range(UNITS + 1):
                    if prep and k == 0:
                        dve.wait_ge(in_loaded[prep.par], 64 * (prep.half + 1))
                        nc.vector.reduce_sum(sev[:, :], cT[prep.par][:, 0:T0], AX.X).then_inc(sev_ready, 1)
                    if rate and k < UNITS:
                        for h, t, c, n in chunks_of(k):
                            dve.wait_ge(sx_full, NMAX * rate.n + n + 1)
                            w = min(CH, NKEY - c * CH)
                            nc.vector.reduce_max(mx[:, h * QT + t, c:c + 1], SX[n % 2][:, 0:w], AX.X).then_inc(sx_read, 1)
                    if prep and k in PREP_SLOT:
                        prep_piece(prep, PREP_SLOT[k])
                    if prep and k == 4:
                        dve.wait_ge(gz_exp, prep.n + 1)
                        nc.vector.tensor_scalar_add(gate[:, :], gate[:, :], 1.0).then_inc(prep_chain, 1)
                        dve.wait_ge(prep_chain, PREP_LINKS * prep.n + 3)
                        nc.vector.reciprocal(gate[:, :], gate[:, :]).then_inc(prep_chain, 1)
                    if prep and k == 20:
                        dve.wait_ge(e0_exp, prep.n + 1)
                        nc.vector.reduce_sum(d0[:, :, :], e0[:, :, :].rearrange("p t (g k) -> p t g k", k=T0), AX.X)\
                            .then_inc(prep_chain, 1)
                        dve.wait_ge(prep_chain, PREP_LINKS * prep.n + 8)
                        nc.vector.reciprocal(d0[:, :, :], d0[:, :, :]).then_inc(prep_chain, 1)
                        dve.wait_ge(prep_chain, PREP_LINKS * prep.n + 9)
                        for s in range(2):
                            for o, n in ((s * HA, HA), (2 * HA + s * HB, HB)):
                                nc.vector.tensor_scalar(d0[:, :, o:o + n], d0[:, :, o:o + n],
                                                        gate[:, s:s + 1], None, mult).then_inc(w0_ready, 1)
                    if rate and k == 26:
                        group_max(rate, 0)
                    if rate and k == UNITS:
                        group_max(rate, 1)
                    if rate and k in RATE_SLOT:
                        rate_piece(rate, RATE_SLOT[k])
                    if rate and k == 22:
                        dve.wait_ge(m1_read, rate_no(rate, "cs3"))
                        nc.vector.reciprocal(cm[:, :], cden[:, :]).then_inc(cden_ready, 1)
                    if rate and k == 45:
                        base = RATE_LINKS * rate.n + 4
                        dve.wait_ge(s2_exp, rate.n + 1)
                        dve.wait_ge(m1_read, rate_no(rate, "sc"))
                        nc.vector.reduce_sum(d2[:, :], p2[:, :, :], AX.X).then_inc(rate_chain, 1)
                        dve.wait_ge(rate_chain, base + 1)
                        nc.vector.reciprocal(d2[:, :], d2[:, :]).then_inc(rate_chain, 1)
                        dve.wait_ge(rate_chain, base + 2)
                        tt(p2[:, :, :], p2[:, :, :], d2[:, :].unsqueeze(2).broadcast_to([NC2, H1, NCA]), mult)\
                            .then_inc(p2_ready, 1)
                    for b, g, at in ((fin, 1, 3), (att, 0, 29)):
                        if b and k == at:
                            dve.wait_ge(fin_full, 3 * b.n + g + 1)
                            wait(dve, out_stored, 16 * b.n)
                            nc.vector.reciprocal(rb[:, g, :], M1[:, 0:S]).then_inc(fin_read, 1)
                    if fin and k == 7:
                        dve.wait_ge(fin_full, 3 * fin.n + 3)
                        dve.wait_ge(res_ready, fin.n + 1)
                        tt(o1, M1[:, 0:QT * D],
                           res[fin.par][:, :, :].rearrange("p t d -> p (t d)"), add).then_inc(fin_read, 1)

            steps(dve, step)

        @block.gpsimd
        def _(pool):
            def tt(o, a, b, op):
                return nc.gpsimd.tensor_tensor(o, a, b, op)

            nc.gpsimd.memset(kspa[0:3, 0, :], 1.0).then_inc(consts, 1)
            for p in range(2):
                nc.gpsimd.memset(v[p][:, :, :, D1 + 1:PAD], 0.0)
                nc.gpsimd.memset(v[p][:, :, :, D1:D1 + 1], 1.0).then_inc(consts, 1)
            pool.wait_ge(w_loaded, 32)

            def split(b, name):
                at = KEYS.index(name)
                n = int(name[-1])
                if len(name) == 2:
                    rows, parts = SPLIT_A, [kspa[:, a, n * CH:(n + 1) * CH] for a in range(3)]
                else:
                    rows, parts = P, [kspb[:, a, n, :] for a in range(3)]
                pool.wait_ge(m0_read, prep_no(b, name))
                on_its_own(pool)
                nc.gpsimd.tensor_copy(parts[1], kr[0:rows, at % 2, :]).then_inc(split_chain, 1)
                pool.wait_ge(split_chain, KQ_LINKS * b.n + at + 1)
                tt(parts[2], kr[0:rows, at % 2, :], parts[1], ALU.subtract).then_inc(ksp_ready, 1)

            def split_queries(b):
                at = KQ_LINKS * b.n + len(KEYS)
                pool.wait_ge(m0_read, prep_no(b, "q1"))
                wait(pool, qscr_done, 32 * b.n)
                on_its_own(pool)
                nc.gpsimd.tensor_copy(qsp[:, 0, :], qs).then_inc(split_chain, 1)
                pool.wait_ge(split_chain, at + 1)
                tt(qr, qs, qsp[:, 0, :], ALU.subtract).then_inc(split_chain, 1)
                pool.wait_ge(split_chain, at + 2)
                on_its_own(pool)
                nc.gpsimd.tensor_copy(qsp[:, 1, :], qr).then_inc(split_chain, 1)
                pool.wait_ge(split_chain, at + 3)
                tt(qsp[:, 2, :], qr, qsp[:, 1, :], ALU.subtract).then_inc(qsp_ready, 1)

            def load_maxima(b, g):
                pool.wait_ge(msp_ready, G * b.n + g + 1)
                wait(pool, m_loaded[g], 16 * b.n)
                on_its_own(pool)
                pool.dma_start(mscr[g].rearrange("a r q -> r a q"), msp[:, :, :]).then_inc(mscr_done, 16)
                pool.wait_ge(mscr_done, 16 * (G * b.n + g + 1))
                on_its_own(pool)
                pool.dma_start(qa[b.par][KR:KR + 3, g * HG:(g + 1) * HG, :],
                               mscr[g].rearrange("a (h t) q -> a h (t q)", t=QT)).then_inc(m_loaded[g], 16)

            def normalise(b, g):
                pool.wait_ge(fin_read, 3 * b.n + g + 1)
                tt(us[:, g, :], us[:, g, :], rb[:, g, :], ALU.mult).then_inc(z_chain, 1)
                pool.wait_ge(z_chain, G * b.n + g + 1)
                tt(us[:, g, :], us[:, g, :], zc[b.par][:, g, :], ALU.add).then_inc(z1_ready, 1)

            def step(prep, rate, att, fin):
                for k in range(UNITS + 1):
                    if prep and k == 0:
                        pool.wait_ge(in_loaded[prep.par], 64 * (prep.half + 1))
                        wait(pool, m0_full, NPREP * (prep.n - 1) + 1)
                        on_its_own(pool)
                        for s, t in enumerate((T0, 0)):
                            last = nc.gpsimd.tensor_copy(
                                tok0[:, s], cT[prep.par][:, t:t + T0].unsqueeze(1).broadcast_to([C, 8, T0]))
                        last.then_inc(tok0_ready, 1)
                    if rate and k == 2:
                        wait(pool, m1_full, NRATE * (rate.n - 1) + RATE.index("ca") + 1)
                        on_its_own(pool)
                        nc.gpsimd.tensor_copy(tok2[:, :, :], cT[rate.par][:, NKEY:NCTX].unsqueeze(1)
                                              .broadcast_to([C, H1, NCA])).then_inc(tok2_ready, 1)
                    if fin and k == 4:
                        normalise(fin, 1)
                    if prep and k == 5:
                        pool.wait_ge(in_loaded[prep.par], 64 * (prep.half + 1))
                        tt(hn[prep.par][:, :, :], hn[prep.par][:, :, :],
                           W("b0n").unsqueeze(1).broadcast_to([P, QT, G * P]), ALU.add).then_inc(xb_ready, 1)
                    if prep and PREP_SLOT.get(k) in KEYS:
                        split(prep, PREP_SLOT[k])
                    if prep and k == 21:
                        pool.wait_ge(w0_ready, 4 * (prep.n + 1))
                        e = e0[:, :, :].rearrange("p t (g k) -> p t g k", k=T0)
                        tt(e, e, d0[:, :, :].unsqueeze(3).broadcast_to([P, QT, 2 * H0, T0]), ALU.mult)\
                            .then_inc(p0_ready, 1)
                    if prep and k == PREP.index("q1") * 2:
                        split_queries(prep)
                    if rate and k == 11:
                        pool.wait_ge(m0_read, prep_no(rate, "hn"))
                        wait(pool, fin_read, 3 * (rate.n - 1))
                        for t in range(QT):
                            last = tt(res[rate.par][:, t, :].rearrange("p (h d) -> p h d", d=D1),
                                      hn[rate.par][:, t, :].rearrange("p (h d) -> p h d", d=PAD)[:, :, 0:D1],
                                      W("b1n").rearrange("p (h d) -> p h d", d=D1), ALU.add)
                        last.then_inc(res_ready, 1)
                    if rate and k == 14:
                        pool.wait_ge(m1_read, rate_no(rate, "caq"))
                        for g in range(G):
                            last = tt(caqb[:, g], caq[:, g, :].unsqueeze(1).broadcast_to([P, HG, NC2]),
                                      W("mask_h").unsqueeze(2).broadcast_to([P, HG, NC2]), ALU.mult)
                        last.then_inc(caqb_ready, 1)
                    if rate and k == 23:
                        pool.wait_ge(cden_ready, rate.n + 1)
                        tt(pc[:, :, :], pc[:, :, :], cm[:, :].unsqueeze(2).broadcast_to([NC2, H1, S]), ALU.mult)\
                            .then_inc(pc_ready, 1)
                    if rate and k == 28:
                        load_maxima(rate, 0)
                    if att and k == 30:
                        normalise(att, 0)
                if rate:
                    load_maxima(rate, 1)

            steps(pool, step)


def kernel(x, ctx_768, L0_xattn_w_q, L0_xattn_w_k, L0_xattn_w_v, L0_xattn_w_k_dis, L0_xattn_w_v_dis,
           L0_xattn_w_gate, L0_xattn_b_gate, L0_xattn_anat_gate_logit, L0_xattn_dis_gate_logit,
           L0_xattn_w_out, L0_xattn_b_out, L1_xattn_Wq, L1_xattn_Wk, L1_xattn_Wv, L1_xattn_Wq_ca,
           L1_xattn_Wk_ca, L1_xattn_Wv_ca, L1_xattn_Wout, L1_xattn_b_out):
    import concourse.bacc as bacc
    from concourse.bass_utils import run_bass_kernel_spmd

    def cols(a):
        a = np.asarray(a)
        out = np.zeros((*a.shape[:-1], G, HG, PAD), a.dtype)
        out[..., :D1] = a.reshape(*a.shape[:-1], G, HG, D1)
        return out.reshape(*a.shape[:-1], G * P)

    def rows(a):
        return cols(np.asarray(a).T).reshape(-1, G, P).transpose(2, 1, 0)

    def table(n, widths, at, items):
        out = np.zeros((n, sum(widths.values())), np.float32)
        for name, a in items.items():
            a = np.asarray(a)
            a = a.reshape(a.shape[0], -1)
            out[:a.shape[0], at[name][0]:at[name][0] + a.shape[1]] = a
        return out

    r = np.arange(P)
    same = lambda a, b: (a[:, None] == b[None, :])
    wo0 = cols(np.asarray(L0_xattn_w_out).T)
    wq1 = rows(L1_xattn_Wq)
    all_rows = lambda a: np.broadcast_to(np.asarray(a), (P, np.size(a)))
    items = dict(
        ident=np.eye(P), b0p=cols(L0_xattn_b_out).reshape(G, P).T, b0n=all_rows(cols(L0_xattn_b_out)),
        b1n=all_rows(L1_xattn_b_out),
        spread=(r[:, None] % PAD == D1) & same(r // PAD, r // PAD),
        mask_a=same(r // D0, np.arange(HA)), mask_b=same(r[:HB * D0] // D0, np.arange(HB)),
        mask_h=same(r // PAD, np.arange(HG)), mask_v=same(r // T0, np.arange(64) // D0),
        mask_v4=same(r % 64 // T0, np.arange(32) // D0),
        logits=np.stack([np.broadcast_to(np.asarray(a).reshape(()), (P,)) for a in (
            L0_xattn_b_gate, L0_xattn_anat_gate_logit, L0_xattn_dis_gate_logit)], 1),
        wq0=rows(np.asarray(L0_xattn_w_q).T), wo0a=wo0[:P], wo0b=wo0[P:],
        wq1=np.concatenate([wq1, np.zeros((P, G, 2 * SPLIT_A - D), np.float32)], 2),
        wqpp=cols(wq1), wo1=rows(L1_xattn_Wout),
        mask_v2=same(np.arange(H1 * NCA) // NCA, np.arange(G * P) // PAD))
    w128 = table(P, W128, O128, items)
    repeat = np.linspace(0, NC2 - 1, S).astype(np.int64)
    items = dict(
        wk0=np.asarray(L0_xattn_w_k).T, wkd0=np.asarray(L0_xattn_w_k_dis).T,
        wv0=np.asarray(L0_xattn_w_v).T, wvd0=np.asarray(L0_xattn_w_v_dis).T,
        wg=np.asarray(L0_xattn_w_gate).T, repeat=same(np.arange(NC2), repeat),
        wk1=L1_xattn_Wk, wv1=L1_xattn_Wv, wkca=cols(L1_xattn_Wk_ca), wvca=cols(L1_xattn_Wv_ca),
        wqca=cols(L1_xattn_Wq_ca))
    w96 = table(C, W96, O96, items)
    xp = cols(x)
    c = np.asarray(ctx_768)
    arrays = {
        "x_t": xp.reshape(B, S, G, P).transpose(0, 3, 2, 1),
        "x_n": xp.reshape(B, QT, P, G * P).transpose(0, 2, 1, 3),
        "ctx_t": c.transpose(0, 2, 1), "ca_n": c[:, NKEY:], "w128": w128, "w96": w96,
    }
    arrays = {n: np.ascontiguousarray(a) for n, a in arrays.items()}
    nc = bacc.Bacc("TRN2", target_bir_lowering=False, num_devices=1)
    aps = [nc.dram_tensor(n, a.shape, mybir.dt.from_np(a.dtype), kind="ExternalInput").ap()
           for n, a in arrays.items()]
    out = nc.dram_tensor("out", (B, S, D), mybir.dt.float32, kind="ExternalOutput").ap()
    program(nc, *aps, out)
    return run_bass_kernel_spmd(nc, [arrays], core_ids=[0]).results[0]["out"]
```

```python
import numpy as np

import concourse.bass as bass
from concourse import mybir
from contextlib import ExitStack

B, S, D, C, NKEY, NCA = 8, 256, 160, 96, 1597, 4
NCTX = NKEY + NCA
P = 128
QT = S // P
H0, D0, T0 = 20, 8, 16
HA = P // D0
HB = H0 - HA
H1, D1 = 8, 20
G, HG = 2, 4
PAD = 32
KT = -(-NKEY // P)
LAST = NKEY - (KT - 1) * P
CH = 400
NCH = 4
KW = CH * NCH
NC2 = 96
CT = H1 * NC2 // P
HALF = 2
UNITS = G * KT * (HG // HALF)
ST = 3
NP = 4
PARTS_K = (0, 0, 0, 1, 1, 2)
PARTS_Q = (0, 1, 2, 0, 1, 0)
TERMS = len(PARTS_K)
KR = TERMS * D1
SPLIT_A = 6 * D1
SPLIT_B = D - SPLIT_A

W128 = dict(ident=128, spread=128, mask_a=HA, mask_b=HB, mask_h=HG, mask_v=64, mask_v4=32, b0p=G,
            b1n=D, logits=3, wq0=G * D, wo0a=G * P, wo0b=G * P, wq1=G * 2 * SPLIT_A,
            wqpp=G * G * P, wo1=G * D, mask_v2=G * P)
W96 = dict(wk0=D, wkd0=D, wv0=D, wvd0=D, wg=1, repeat=S, wk1=SPLIT_A + 64, wv1=D, wkca=G * P,
           wvca=G * P, wqca=G * P)


def offsets(table):
    at, out = 0, {}
    for name, n in table.items():
        out[name] = (at, at + n)
        at += n
    return out, at


O128, N128 = offsets(W128)
O96, N96 = offsets(W96)

PREP_SLOT = {0: "small", 2: "q0", 4: "s0", 6: "s1", 8: "s2", 10: "k0", 12: "k1", 14: "k2",
             16: "t0", 18: "t1", 20: "t2", 22: "z", 25: "h", 28: "q1", 30: "k3", 32: "kb0",
             34: "kb1", 37: "hn"}
PREP = [PREP_SLOT[n] for n in sorted(PREP_SLOT)]
RATE_SLOT = {2: "ca", 4: "caq", 8: "v0", 10: "cs0", 12: "cs1", 16: "cs2", 18: "v1", 20: "v2",
             22: "v3", 24: "ct0", 26: "ct1", 28: "m0", 30: "ct2", 32: "v4", 34: "c1", 36: "c2",
             40: "sc", 44: "pe", 46: "zc", 51: "m1"}
RATE = [RATE_SLOT[n] for n in sorted(RATE_SLOT)]
DEN1, OUT, DEN0 = 6, 14, 38
MAX_SLOTS = 47
NRATE, NPREP = len(RATE), len(PREP)
KEYS = ["k0", "k1", "k2", "k3", "kb0", "kb1"]
NMAX = H1 * QT * NCH
PREP_LINKS = 9
RATE_LINKS = 9
KSTORES = 7


class Batch:

    def __init__(self, i, c):
        self.i, self.c, self.par = i, c, c % 2

    @property
    def n(self):
        return 2 * self.i + self.c

    @property
    def half(self):
        return self.i + self.c // 2


def wait(eng, sem, value):
    if not (isinstance(value, int) and value <= 0):
        eng.wait_ge(sem, value)


def steps(eng, step):
    one = lambda c: Batch(0, c)
    step(one(0), None, None, None)
    step(one(1), one(0), None, None)
    step(one(2), one(1), one(0), None)
    with eng.Fori(0, 2) as i:
        for c in (1, 2):
            step(Batch(i, c + 2), Batch(i, c + 1), Batch(i, c), Batch(i, c - 1))
    step(one(7), one(6), one(5), one(4))
    step(None, one(7), one(6), one(5))
    step(None, None, one(7), one(6))
    step(None, None, None, one(7))


def program(nc, x_t, ctx_t, ca_n, w128, w96, out):
    fp32, bf16 = mybir.dt.float32, mybir.dt.bfloat16
    ALU, ACT, AX = mybir.AluOpType, mybir.ActivationFunctionType, mybir.AxisListType
    SC0 = 1.0 / float(np.sqrt(D0))
    SC1 = float(D1) ** -0.5

    ctx = ExitStack()
    with ctx:
        def sb(name, shape, dt=fp32):
            return ctx.enter_context(nc.sbuf_tensor(name, shape, dt))

        def sem(name):
            return ctx.enter_context(nc.semaphore(name))

        wp = sb("wp", [P, N128])
        wc = sb("wc", [C, N96])

        def W(name, rows=P):
            return wp[0:rows, O128[name][0]:O128[name][1]]

        def Wc(name, rows=C):
            return wc[0:rows, O96[name][0]:O96[name][1]]

        cT = [sb(f"cT{p}", [C, NCTX]) for p in range(2)]
        can = [sb(f"can{p}", [NCA, C]) for p in range(2)]
        sev = sb("sev", [C, 1])
        tok0 = sb("tok0", [C, 2, 8, T0])
        tok2 = sb("tok2", [C, H1, NCA])
        gz = sb("gz", [P, 2])
        gate = sb("gate", [P, 2])
        kb0a = sb("kb0a", [P, 2, HA, T0])
        kb0b = sb("kb0b", [HB * D0, 2, HB, T0])
        vb0 = sb("vb0", [P, 4, 64])
        vb4 = sb("vb4", [P, 32])
        q0a = sb("q0a", [P, S])
        q0b = sb("q0b", [HB * D0, S])
        e0 = sb("e0", [P, QT, 2 * H0 * T0])
        m0x = sb("m0x", [P, QT, 2 * H0])
        d0 = sb("d0", [P, QT, 2 * H0])
        pT0 = sb("pT0", [P, 5, S])
        z0a = sb("z0a", [P, S])
        z0b = sb("z0b", [HB * D0, S])
        hT = [sb(f"hT{p}", [P, G, S]) for p in range(2)]
        hn = [sb(f"hn{p}", [P, QT, G * P]) for p in range(2)]
        res = [sb(f"res{p}", [P, QT, D]) for p in range(2)]
        qs = e0[0:SPLIT_A, 0, 0:2 * S]
        qsp = sb("qsp", [SPLIT_A, 3, 2 * S], bf16)
        kr = sb("kr", [P, 2, CH])
        qr = sb("qr", [SPLIT_A, 2 * S])
        kspa = sb("kspa", [SPLIT_A, 3, KW], bf16)
        kspb = sb("kspb", [P, 3, 2, CH], bf16)
        ka = [sb(f"ka{p}", [KR + 3, H1, KW], bf16) for p in range(2)]
        qa = [sb(f"qa{p}", [KR + 3, H1, S], bf16) for p in range(2)]
        mx = sb("mx", [P, H1 * QT, NCH])
        nm = sb("nm", [P, H1 * QT])
        mr = sb("mr", [HG * QT, P])
        msp = sb("msp", [HG * QT, 3, P], bf16)
        v = [sb(f"v{p}", [P, KT, H1, PAD]) for p in range(2)]
        pr = sb("pr", [P, NP, HALF * S])
        k2b = sb("k2b", [P, G, HG, NCA])
        v2b = sb("v2b", [H1 * NCA, G * P])
        caq = sb("caq", [P, G, NC2])
        caqb = sb("caqb", [P, G, HG, NC2])
        cm = sb("cm", [P, CT])
        cden = sb("cden", [P, CT])
        pc = sb("pc", [P, CT, S])
        pcT = sb("pcT", [P, QT, CT * P])
        c1T = sb("c1T", [P, G, NC2])
        c2T = sb("c2T", [P, G, NC2])
        p2 = sb("p2", [NC2, H1, NCA])
        m2 = sb("m2", [NC2, H1])
        d2 = sb("d2", [NC2, H1])
        p2e = sb("p2e", [H1 * NCA, S])
        zc = [sb(f"zc{p}", [P, G, S]) for p in range(2)]
        us = sb("us", [P, G, S])
        rb = sb("rb", [P, G, S])
        o1 = rb[:, :, :].rearrange("p g s -> p (g s)")[:, 0:QT * D]

        bank = [ctx.enter_context(nc.psum_tensor(f"bank{n}", [P, 512], fp32)) for n in range(8)]
        U, SX, M0, M1 = bank[3], bank[4:6], bank[6], bank[7]

        kscr = nc.dram_tensor("kscr", (2, 3, D, KW), bf16).ap()
        qscr = nc.dram_tensor("qscr", (2, 3, D, S), bf16).ap()
        mscr = nc.dram_tensor("mscr", (G, 3, HG * QT, P), bf16).ap()

        w_loaded = sem("w_loaded")
        in_loaded = [sem(f"in_loaded{p}") for p in range(2)]
        ones_loaded = sem("ones_loaded")
        consts = sem("consts")
        m0_full, m0_read = sem("m0_full"), sem("m0_read")
        m1_full, m1_read = sem("m1_full"), sem("m1_read")
        fin_full, fin_read = sem("fin_full"), sem("fin_read")
        sev_ready = sem("sev_ready")
        gz_ready, gz_exp = sem("gz_ready"), sem("gz_exp")
        prep_chain = sem("prep_chain")
        rate_chain = sem("rate_chain")
        split_chain = sem("split_chain")
        query_chain = sem("query_chain")
        z_chain = sem("z_chain")
        e0_exp, w0_ready, p0_ready = sem("e0_exp"), sem("w0_ready"), sem("p0_ready")
        tok0_ready, tok2_ready = sem("tok0_ready"), sem("tok2_ready")
        k1_ready = sem("k1_ready")
        ksp_ready, qsp_ready = sem("ksp_ready"), sem("qsp_ready")
        kscr_done, qscr_done = sem("kscr_done"), sem("qscr_done")
        kq_loaded = [[sem(f"kq_loaded{p}{g}") for g in range(G)] for p in range(2)]
        sx_full, sx_read = sem("sx_full"), sem("sx_read")
        msp_ready = sem("msp_ready")
        mscr_done = sem("mscr_done")
        m_loaded = [sem(f"m_loaded{g}") for g in range(G)]
        st_full, exp_done, pv_done = sem("st_full"), sem("exp_done"), sem("pv_done")
        caqb_ready, cm_ready = sem("caqb_ready"), sem("cm_ready")
        cden_ready, pc_ready = sem("cden_ready"), sem("pc_ready")
        s2_exp, p2_ready = sem("s2_exp"), sem("p2_ready")
        res_ready = sem("res_ready")
        u_read, z1_ready = sem("u_read"), sem("z1_ready")
        out_stored = sem("out_stored")
        passed = sem("passed")

        prep_no = lambda b, name: NPREP * b.n + PREP.index(name) + 1
        rate_no = lambda b, name: NRATE * b.n + RATE.index(name) + 1

        def chunks_of(k):
            return [(n // (QT * NCH), n // NCH % QT, n % NCH, n)
                    for n in range(NMAX) if n * MAX_SLOTS // NMAX == k]

        def unit(k):
            return k // (KT * 2), k // 2 % KT, k % 2

        def st_bank(b, k):
            return bank[(k + b.par) % ST]

        def last_use(b, k):
            if k >= ST:
                return k - ST
            return next(n for n in (-1, -2, -3) if (UNITS + n + 1 - b.par) % ST == (k + b.par) % ST)

        def on_its_own(eng):
            eng.sem_inc(passed, 1)

        block = ctx.enter_context(nc.Block())

        def load_inputs(eng, b):
            p = b.par
            eng.dma_start(cT[p][:, :], ctx_t[bass.ds(b.n, 1)].rearrange("a c n -> (a c) n"))\
              .then_inc(in_loaded[p], 16)
            eng.dma_start(hT[p][:, :, :], x_t[bass.ds(b.n, 1)].rearrange("a p g s -> (a p) g s"))\
              .then_inc(in_loaded[p], 16)
            eng.dma_start(can[p][:, :], ca_n[bass.ds(b.n, 1)].rearrange("a t c -> (a t) c"))\
              .then_inc(in_loaded[p], 16)

        @block.sync
        def _(sp):
            load_inputs(sp, Batch(0, 0))
            sp.dma_start(wc[:, :], w96).then_inc(w_loaded, 16)
            sp.dma_start(wp[:, :], w128).then_inc(w_loaded, 16)
            sp.wait_ge(consts, 1)
            for p in range(2):
                sp.dma_start(ka[p][KR:KR + 3, :, :], kspa[0:3, 0:1, :].broadcast_to([3, H1, KW]))\
                  .then_inc(ones_loaded, 16)

            def load_parts(b, g, stack, scr, parts):
                wait(sp, st_full, UNITS * (b.n - 2) + (g + 1) * (UNITS // G))
                on_its_own(sp)
                for t in range(TERMS):
                    src = scr[b.par, parts[t]].rearrange("(g h d) n -> g d h n", g=G, h=HG)[g]
                    sp.dma_start(stack[b.par][t * D1:(t + 1) * D1, g * HG:(g + 1) * HG, :], src)\
                      .then_inc(kq_loaded[b.par][g], 16)

            def step(prep, rate, att, fin):
                if rate:
                    load_parts(rate, 1, qa, qscr, PARTS_Q)
                    load_parts(rate, 1, ka, kscr, PARTS_K)
                if fin:
                    sp.wait_ge(fin_read, 3 * (fin.n + 1))
                    on_its_own(sp)
                    sp.dma_start(out[bass.ds(fin.n, 1)].rearrange("a (t q) d -> q (a t) d", q=P),
                                 o1.rearrange("p (t d) -> p t d", t=QT)).then_inc(out_stored, 16)
                if prep:
                    wait(sp, kq_loaded[prep.par][1], 16 * 2 * TERMS * prep.half)
                    on_its_own(sp)
                    sp.wait_ge(qsp_ready, prep.n + 1)
                    on_its_own(sp)
                    dst = qscr[prep.par].rearrange("a r n -> r a n")
                    sp.dma_start(dst[0:SPLIT_A], qsp[:, :, 0:S]).then_inc(qscr_done, 16)
                    sp.dma_start(dst[SPLIT_A:D], qsp[0:SPLIT_B, :, S:2 * S]).then_inc(qscr_done, 16)
                    sp.wait_ge(qscr_done, 32 * (prep.n + 1))
                    on_its_own(sp)
                    load_parts(prep, 0, qa, qscr, PARTS_Q)
                    sp.wait_ge(ksp_ready, len(KEYS) * prep.n + NCH)
                    on_its_own(sp)
                    sp.dma_start(kscr[prep.par].rearrange("a r n -> r a n")[0:SPLIT_A], kspa[:, :, :])\
                      .then_inc(kscr_done, 16)
                    sp.wait_ge(ksp_ready, len(KEYS) * (prep.n + 1))
                    on_its_own(sp)
                    for u in range(2):
                        for a in range(3):
                            dst = kscr[prep.par, a, SPLIT_A:D].rearrange("r (c u n) -> u r c n", c=2, u=2)[u]
                            sp.dma_start(dst, kspb[64 * u:64 * u + SPLIT_B, a, :, :]).then_inc(kscr_done, 16)
                    sp.wait_ge(kscr_done, 16 * KSTORES * (prep.n + 1))
                    on_its_own(sp)
                    load_parts(prep, 0, ka, kscr, PARTS_K)

            load_inputs(sp, Batch(0, 1))
            steps(sp, step)
            sp.wait_ge(out_stored, 16 * B)

        @block.tensor
        def _(pe):
            def mm(o, lhs, rhs, start=True, stop=True):
                return nc.tensor.matmul(o, lhs, rhs, start=start, stop=stop)

            pe.wait_ge(w_loaded, 32)
            pe.wait_ge(consts, 3)
            pe.wait_ge(ones_loaded, 32)
            tok = [slice(T0, 2 * T0), slice(0, T0)]
            tail = slice(NKEY, NCTX)

            def prep_piece(b, name):
                p, at = b.par, PREP.index(name)
                wait(pe, m0_read, NPREP * b.n + at)
                wk = [Wc("wk0"), Wc("wkd0")]
                wv = [Wc("wv0"), Wc("wvd0")]
                if name == "small":
                    pe.wait_ge(in_loaded[p], 48 * (b.half + 1))
                    pe.wait_ge(tok0_ready, b.n + 1)
                    for s in range(2):
                        r8 = tok0[:, s, :, :].rearrange("p h k -> p (h k)")
                        t = cT[p][:, tok[s]]
                        mm(M0[:, s * T0:(s + 1) * T0], wk[s][:, 0:P], t)
                        mm(M0[0:HB * D0, 32 + s * T0:32 + (s + 1) * T0], wk[s][:, P:D], t)
                        for u in range(2):
                            c = 2 * s + u
                            mm(M0[:, 64 + 64 * c:128 + 64 * c],
                               r8, wv[s][:, 64 * u:64 * u + 64])
                        mm(M0[64 * s:64 * s + 64, 320:352],
                           r8[:, 0:HB * T0], wv[s][:, P:D])
                    pe.wait_ge(sev_ready, b.n + 1)
                    last = mm(M0[:, 352:353], Wc("wg").broadcast_to([C, P]), sev[:, :])
                elif name == "q0":
                    for cols, o in ((slice(0, P), M0[:, 0:S]), (slice(P, D), M0[0:HB * D0, S:2 * S])):
                        for g in range(G):
                            last = mm(o, W("wq0").rearrange("p (g d) -> p g d", g=G)[:, g, cols],
                                      hT[p][:, g, :], g == 0, g == G - 1)
                elif name in ("k0", "k1", "k2", "k3"):
                    c = int(name[1])
                    last = mm(M0[0:SPLIT_A, 0:CH], Wc("wk1")[:, 0:SPLIT_A], cT[p][:, c * CH:(c + 1) * CH])
                elif name in ("kb0", "kb1"):
                    for u in range(2):
                        c = 2 * int(name[2]) + u
                        last = mm(M0[64 * u:64 * u + 64, 0:CH], Wc("wk1")[:, SPLIT_A:SPLIT_A + 64],
                                  cT[p][:, c * CH:(c + 1) * CH])
                elif name in ("s0", "s1"):
                    t = int(name[1])
                    last = mm(M0[:, :], q0a[:, t * P:(t + 1) * P], kb0a[:, :, :, :].rearrange("p s h k -> p (s h k)"))
                elif name == "s2":
                    for t in range(QT):
                        last = mm(M0[:, t * P:(t + 1) * P], q0b[:, t * P:(t + 1) * P],
                                  kb0b[:, :, :, :].rearrange("p s h k -> p (s h k)"))
                elif name in ("t0", "t1", "t2"):
                    pe.wait_ge(p0_ready, b.n + 1)
                    for c in range(2 * int(name[1]), min(2 * int(name[1]) + 2, 5)):
                        for t in range(QT):
                            o = (c % 2) * S + t * P
                            last = nc.tensor.transpose(M0[:, o:o + P], e0[:, t, c * P:(c + 1) * P], W("ident"))
                elif name == "z":
                    for u in range(2):
                        for s in range(2):
                            mm(M0[64 * u:64 * u + 64, 0:S], vb0[:, 2 * s + u, :], pT0[:, 2 * s + u, :],
                               s == 0, s == 1)
                    last = mm(M0[0:32, S:2 * S], vb4[:, :], pT0[:, 4, :])
                elif name == "h":
                    for g in range(G):
                        o = M0[:, g * S:(g + 1) * S]
                        mm(o, W("wo0a")[:, g * P:(g + 1) * P], z0a[:, :], True, False)
                        last = mm(o, W("wo0b", 32)[:, g * P:(g + 1) * P], z0b[:, :], False, True)
                elif name == "hn":
                    for t in range(QT):
                        for g in range(G):
                            last = nc.tensor.transpose(M0[:, (t * G + g) * P:(t * G + g + 1) * P],
                                                       hT[p][:, g, t * P:(t + 1) * P], W("ident"))
                elif name == "q1":
                    w = W("wq1").rearrange("p (g d) -> p g d", g=G)
                    for u in range(2):
                        for g in range(G):
                            last = mm(M0[0:SPLIT_A, u * S:(u + 1) * S], w[:, g, u * SPLIT_A:(u + 1) * SPLIT_A],
                                      hT[p][:, g, :], g == 0, g == G - 1)
                last.then_inc(m0_full, 1)

            def rate_piece(b, name):
                p, at = b.par, RATE.index(name)
                wait(pe, m1_read, NRATE * b.n + at)
                if name[0] == "v":
                    for t in range(3 * int(name[1]), min(3 * int(name[1]) + 3, KT)):
                        rows = P if t < KT - 1 else LAST
                        o = (t % 3) * D
                        last = mm(M1[0:rows, o:o + D], cT[p][:, t * P:t * P + rows], Wc("wv1"))
                elif name == "ca":
                    for g in range(G):
                        mm(M1[:, g * NCA:(g + 1) * NCA], Wc("wkca")[:, g * P:(g + 1) * P], cT[p][:, tail])
                    pe.wait_ge(tok2_ready, b.n + 1)
                    last = mm(M1[0:H1 * NCA, S:2 * S], tok2[:, :, :].rearrange("p h k -> p (h k)"),
                              Wc("wvca"))
                elif name == "caq":
                    for g in range(G):
                        last = mm(M1[:, g * NC2:(g + 1) * NC2], Wc("wqca", NCA)[:, g * P:(g + 1) * P],
                                  can[p][:, :])
                elif name[:2] == "cs":
                    pe.wait_ge(caqb_ready, b.n + 1)
                    for u in range(2):
                        g, m = divmod(2 * int(name[2]) + u, CT // G)
                        last = mm(M1[:, u * S:(u + 1) * S],
                                  caqb[:, g].rearrange("p h c -> p (h c)")[:, m * P:(m + 1) * P],
                                  hT[p][:, g, :])
                elif name[:2] == "ct":
                    pe.wait_ge(pc_ready, b.n + 1)
                    for n in range(4):
                        m, t = 2 * int(name[2]) + n // 2, n % 2
                        last = nc.tensor.transpose(M1[:, n * P:(n + 1) * P], pc[:, m, t * P:(t + 1) * P],
                                                   W("ident"))
                elif name == "c1":
                    for g in range(G):
                        for t in range(QT):
                            for j in range(HG):
                                last = mm(M1[PAD * j:PAD * (j + 1), g * NC2:(g + 1) * NC2],
                                          hn[p][:, t, g * P + PAD * j:g * P + PAD * (j + 1)],
                                          pcT[:, t, (g * HG + j) * NC2:(g * HG + j + 1) * NC2],
                                          t == 0, t == QT - 1)
                elif name == "c2":
                    w = W("wqpp").rearrange("p (a g d) -> p a g d", a=G, g=G)
                    for g in range(G):
                        for a in range(G):
                            last = mm(M1[:, g * NC2:(g + 1) * NC2], w[:, a, g, :], c1T[:, a, :],
                                      a == 0, a == G - 1)
                elif name == "sc":
                    for g in range(G):
                        last = mm(M1[0:NC2, g * HG * NCA:(g + 1) * HG * NCA], c2T[:, g, :],
                                  k2b[:, g, :, :].rearrange("p h t -> p (h t)"))
                elif name == "pe":
                    pe.wait_ge(p2_ready, b.n + 1)
                    last = mm(M1[0:H1 * NCA, 0:S], p2[:, :, :].rearrange("p h t -> p (h t)"),
                              Wc("repeat", NC2))
                elif name == "zc":
                    for g in range(G):
                        last = mm(M1[:, g * S:(g + 1) * S], v2b[:, g * P:(g + 1) * P], p2e[:, :])
                else:
                    g = int(name[1])
                    pe.wait_ge(rate_chain, RATE_LINKS * b.n + (1, 7)[g])
                    n = HG * QT
                    last = nc.tensor.transpose(M1[0:n, 0:P], nm[:, g * n:(g + 1) * n], W("ident"))
                last.then_inc(m1_full, 1)

            def max_scores(b, k):
                p = b.par
                for h, t, c, n in chunks_of(k):
                    if n % (HG * QT * NCH) == 0:
                        pe.wait_ge(kq_loaded[p][h // HG], 16 * 2 * TERMS * (b.half + 1))
                    wait(pe, sx_read, NMAX * b.n + n - 1)
                    w = min(CH, NKEY - c * CH)
                    mm(SX[n % 2][:, 0:w], qa[p][0:KR, h, t * P:(t + 1) * P], ka[p][0:KR, h, c * CH:c * CH + w])\
                        .then_inc(sx_full, 1)

            def scores(b, k):
                p = b.par
                g, t, u = unit(k)
                if k % (UNITS // G) == 0:
                    pe.wait_ge(m_loaded[g], 16 * (b.n + 1))
                wait(pe, exp_done, UNITS * b.n + last_use(b, k) + 1)
                rows = P if t < KT - 1 else LAST
                for j in range(HALF):
                    h = g * HG + HALF * u + j
                    last = mm(st_bank(b, k)[0:rows, j * S:(j + 1) * S], ka[p][:, h, t * P:t * P + rows],
                              qa[p][:, h, :])
                last.then_inc(st_full, 1)

            def values(b, k):
                p = b.par
                g, t, u = unit(k)
                if k % (UNITS // G) == 0:
                    if g == 0:
                        pe.wait_ge(m1_read, rate_no(b, "v4"))
                    wait(pe, u_read, G * b.n + g)
                pe.wait_ge(exp_done, UNITS * b.n + k + 1)
                rows = P if t < KT - 1 else LAST
                if rows < P:
                    on_its_own(pe)
                for j in range(HALF):
                    q = HALF * u + j
                    last = mm(U[PAD * q:PAD * (q + 1), g * S:(g + 1) * S], v[p][0:rows, t, g * HG + q, :],
                              pr[0:rows, k % NP, j * S:(j + 1) * S], t == 0, t == KT - 1)
                last.then_inc(pv_done, 1)

            def denominators(b, g):
                pe.wait_ge(u_read, G * b.n + g + 1)
                wait(pe, fin_read, 3 * b.n + g)
                mm(M1[:, 0:S], W("spread"), us[:, g, :]).then_inc(fin_full, 1)

            def project(b):
                pe.wait_ge(z1_ready, G * (b.n + 1))
                pe.wait_ge(fin_read, 3 * b.n + 2)
                for t in range(QT):
                    for g in range(G):
                        last = mm(M1[:, t * D:(t + 1) * D], us[:, g, t * P:(t + 1) * P],
                                  W("wo1").rearrange("p (g d) -> p g d", g=G)[:, g, :], g == 0, g == G - 1)
                last.then_inc(fin_full, 1)

            def step(prep, rate, att, fin):
                for k in range(UNITS):
                    if att:
                        scores(att, k)
                        if k % 2 and k > 2:
                            values(att, k - 3)
                            values(att, k - 2)
                    if prep and k in PREP_SLOT:
                        prep_piece(prep, PREP_SLOT[k])
                    if rate and k in RATE_SLOT:
                        if fin and k > DEN1:
                            pe.wait_ge(fin_read, 3 * fin.n + (2 if k < OUT else 3))
                        if att and k > DEN0:
                            pe.wait_ge(fin_read, 3 * att.n + 1)
                        rate_piece(rate, RATE_SLOT[k])
                    if fin and k in (DEN1, OUT) or att and k == DEN0:
                        before = RATE[sum(n < k for n in RATE_SLOT) - 1]
                        pe.wait_ge(m1_read, rate_no(rate, before) if rate else NRATE * B)
                    if fin and k == DEN1:
                        denominators(fin, 1)
                    if fin and k == OUT:
                        project(fin)
                    if att and k == DEN0:
                        denominators(att, 0)
                    if rate:
                        max_scores(rate, k)
                if att:
                    values(att, UNITS - 2)
                    values(att, UNITS - 1)

            steps(pe, step)

        @block.scalar
        def _(act):
            def f(o, i, func=ACT.Copy, **kw):
                return nc.scalar.activation(o, i, func, **kw)

            def prep_piece(b, name):
                if name in ("k0", "k1", "k2", "k3", "kb0", "kb1"):
                    act.wait_ge(m0_full, prep_no(b, name))
                    wait(act, kscr_done, 16 * KSTORES * b.n)
                    n = int(name[-1])
                    if len(name) == 2:
                        f(kspa[:, 0, n * CH:(n + 1) * CH], M0[0:SPLIT_A, 0:CH]).then_inc(k1_ready, 1)
                    else:
                        f(kspb[:, 0, n, :], M0[:, 0:CH]).then_inc(k1_ready, 1)
                elif name == "q0":
                    act.wait_ge(m0_full, prep_no(b, name))
                    f(q0a[:, :], M0[:, 0:S], scale=SC0)
                    f(q0b[:, :], M0[0:HB * D0, S:2 * S], scale=SC0).then_inc(m0_read, 1)
                elif name in ("t0", "t1", "t2"):
                    act.wait_ge(m0_full, prep_no(b, name))
                    n = int(name[1])
                    w = 1 if n == 2 else 2
                    f(pT0[:, 2 * n:2 * n + w, :].rearrange("p a s -> p (a s)"), M0[:, 0:w * S]).then_inc(m0_read, 1)
                elif name == "z":
                    act.wait_ge(m0_full, prep_no(b, name))
                    f(z0a[:, :], M0[:, 0:S])
                    f(z0b[:, :], M0[0:32, S:2 * S]).then_inc(m0_read, 1)
                elif name == "hn":
                    act.wait_ge(m0_full, prep_no(b, name))
                    f(hn[b.par][:, :, :].rearrange("p t d -> p (t d)"), M0[:, :]).then_inc(m0_read, 1)
                elif name == "q1":
                    act.wait_ge(m0_full, prep_no(b, name))
                    wait(act, qsp_ready, b.n)
                    f(qs, M0[0:SPLIT_A, :], scale=SC1).then_inc(m0_read, 1)

            def rate_piece(b, name):
                p = b.par
                if name[0] == "v":
                    act.wait_ge(m1_full, rate_no(b, name))
                    wait(act, pv_done, UNITS * (b.n - 1))
                    n = int(name[1])
                    t0, t1 = 3 * n, min(3 * n + 3, KT)
                    rows = P if t1 < KT else LAST
                    f(v[p][0:rows, t0:t1, :, 0:D1],
                      M1[0:rows, 0:(t1 - t0) * D].rearrange("p (t h d) -> p t h d", h=H1, d=D1))\
                        .then_inc(m1_read, 1)
                elif name == "caq":
                    act.wait_ge(m1_full, rate_no(b, name))
                    wait(act, caqb_ready, b.n)
                    f(caq[:, :, :].rearrange("p g c -> p (g c)"), M1[:, 0:G * NC2], scale=SC1).then_inc(m1_read, 1)
                elif name[:2] == "cs":
                    n = int(name[2])
                    act.wait_ge(cm_ready, CT // 2 * b.n + n + 1)
                    for u in range(2):
                        h = 2 * n + u
                        last = f(pc[:, h, :], M1[:, u * S:(u + 1) * S], ACT.Exp, bias=cm[:, h:h + 1],
                                 accum_out=cden[:, h:h + 1])
                    last.then_inc(m1_read, 1)
                elif name[:2] == "ct":
                    act.wait_ge(m1_full, rate_no(b, name))
                    n = int(name[2])
                    f(pcT[:, :, 2 * n * P:(2 * n + 2) * P].rearrange("p t (u c) -> p u t c", u=2),
                      M1[:, :].rearrange("p (u t c) -> p u t c", u=2, t=QT)).then_inc(m1_read, 1)
                elif name == "c1":
                    act.wait_ge(m1_full, rate_no(b, name))
                    f(c1T[:, :, :].rearrange("p g c -> p (g c)"), M1[:, 0:G * NC2]).then_inc(m1_read, 1)
                elif name == "c2":
                    act.wait_ge(m1_full, rate_no(b, name))
                    f(c2T[:, :, :].rearrange("p g c -> p (g c)"), M1[:, 0:G * NC2], scale=SC1).then_inc(m1_read, 1)
                elif name == "pe":
                    act.wait_ge(m1_full, rate_no(b, name))
                    f(p2e[:, :], M1[0:H1 * NCA, 0:S]).then_inc(m1_read, 1)
                elif name == "zc":
                    act.wait_ge(m1_full, rate_no(b, name))
                    wait(act, z1_ready, G * (b.n - 1))
                    f(zc[p][:, :, :].rearrange("p g s -> p (g s)"), M1[:, :]).then_inc(m1_read, 1)

            def copy_u(b, g):
                act.wait_ge(pv_done, UNITS * b.n + (g + 1) * (UNITS // G))
                wait(act, fin_full, 3 * b.n)
                f(us[:, g, :], U[:, g * S:(g + 1) * S]).then_inc(u_read, 1)

            def step(prep, rate, att, fin):
                if fin:
                    copy_u(fin, 1)
                for n in range(UNITS + 1):
                    k = n - 1
                    if prep and k in PREP_SLOT:
                        prep_piece(prep, PREP_SLOT[k])
                    if prep and k == 1:
                        act.wait_ge(gz_ready, prep.n + 1)
                        f(gate[:, :], gz[:, :], ACT.Exp).then_inc(gz_exp, 1)
                    if prep and k == 9:
                        act.wait_ge(m0_read, prep_no(prep, "s2"))
                        e = e0[:, :, :].rearrange("p t n -> p (t n)")
                        f(e, e, ACT.Exp).then_inc(e0_exp, 1)
                    if rate and k in RATE_SLOT:
                        rate_piece(rate, RATE_SLOT[k])
                    if rate and k == 41:
                        act.wait_ge(m1_read, rate_no(rate, "sc"))
                        e = p2[:, :, :].rearrange("p h t -> p (h t)")
                        f(e, e, ACT.Exp).then_inc(s2_exp, 1)
                    if rate and prep and k == 33:
                        if not (isinstance(prep.n, int) and prep.n == B - 1):
                            act.wait_ge(m1_full, rate_no(rate, "v4"))
                            on_its_own(act)
                            act.wait_ge(res_ready, rate.n + 1)
                            on_its_own(act)
                            load_inputs(act, Batch(prep.i, prep.c + 1))
                    if att and k == 27:
                        copy_u(att, 0)
                    if att and n < UNITS:
                        act.wait_ge(st_full, UNITS * att.n + n + 1)
                        wait(act, pv_done, UNITS * att.n + n - NP + 1)
                        rows = P if unit(n)[1] < KT - 1 else LAST
                        f(pr[0:rows, n % NP, :], st_bank(att, n)[0:rows, :], ACT.Exp).then_inc(exp_done, 1)

            act.wait_ge(ones_loaded, 32)
            steps(act, step)

        @block.vector
        def _(dve):
            dve.wait_ge(w_loaded, 32)
            mult, add, sub = ALU.mult, ALU.add, ALU.subtract

            def tt(o, a, b, op):
                return nc.vector.tensor_tensor(o, a, b, op)

            def prep_piece(b, name):
                p = b.par
                full = lambda: dve.wait_ge(m0_full, prep_no(b, name))
                if name == "small":
                    full()
                    lg = W("logits")
                    at = PREP_LINKS * b.n
                    nc.vector.tensor_scalar(gz[:, 0:1], M0[:, 352:353], 1.0 / T0, lg[:, 0:1], mult, add)\
                        .then_inc(prep_chain, 1)
                    dve.wait_ge(prep_chain, at + 1)
                    nc.vector.tensor_scalar(gz[:, 1:2], gz[:, 0:1], -1.0, lg[:, 2:3], mult, sub)\
                        .then_inc(prep_chain, 1)
                    dve.wait_ge(prep_chain, at + 2)
                    tt(gz[:, 0:1], gz[:, 0:1], lg[:, 1:2], sub).then_inc(gz_ready, 1)
                    for s in range(2):
                        tt(kb0a[:, s], M0[:, s * T0:(s + 1) * T0].unsqueeze(1).broadcast_to([P, HA, T0]),
                           W("mask_a").unsqueeze(2).broadcast_to([P, HA, T0]), mult)
                        tt(kb0b[:, s],
                           M0[0:32, 32 + s * T0:32 + (s + 1) * T0].unsqueeze(1).broadcast_to([32, HB, T0]),
                           W("mask_b", 32).unsqueeze(2).broadcast_to([32, HB, T0]), mult)
                    tt(vb0[:, :, :], M0[:, 64:320].rearrange("p (c n) -> p c n", c=4),
                       W("mask_v").unsqueeze(1).broadcast_to([P, 4, 64]), mult)
                    tt(vb4[:, :], M0[:, 320:352], W("mask_v4"), mult).then_inc(m0_read, 1)
                elif name[0] == "k":
                    full()
                    n = int(name[-1])
                    at = KEYS.index(name)
                    dve.wait_ge(k1_ready, len(KEYS) * b.n + at + 1)
                    wait(dve, ksp_ready, len(KEYS) * b.n + at - 1)
                    first = kspa[:, 0, n * CH:(n + 1) * CH] if len(name) == 2 else kspb[:, 0, n, :]
                    rows = SPLIT_A if len(name) == 2 else P
                    tt(kr[0:rows, at % 2, :], M0[0:rows, 0:CH], first, sub).then_inc(m0_read, 1)
                elif name in ("s0", "s1", "s2"):
                    full()
                    wait(dve, qsp_ready, b.n)
                    n = int(name[1])
                    wait(dve, m0_read, NPREP * (b.n - 1) + PREP.index("t2") + 1)
                    if n < 2:
                        src = M0[:, :].rearrange("p (g k) -> p g k", k=T0)
                        dst = e0[:, n, 0:512].rearrange("p (g k) -> p g k", k=T0)
                        m = m0x[:, n, 0:2 * HA]
                        mb = m.unsqueeze(2).broadcast_to([P, 2 * HA, T0])
                    else:
                        src = M0[:, 0:256].rearrange("p (t g k) -> p t g k", t=QT, k=T0)
                        dst = e0[:, :, 512:640].rearrange("p t (g k) -> p t g k", k=T0)
                        m = m0x[:, :, 2 * HA:2 * H0]
                        mb = m.unsqueeze(3).broadcast_to([P, QT, 2 * HB, T0])
                    nc.vector.reduce_max(m, src, AX.X).then_inc(prep_chain, 1)
                    dve.wait_ge(prep_chain, PREP_LINKS * b.n + 5 + n)
                    tt(dst, src, mb, sub).then_inc(m0_read, 1)
                elif name == "h":
                    full()
                    for g in range(G):
                        last = nc.vector.scalar_tensor_tensor(out=hT[p][:, g, :], in0=M0[:, g * S:(g + 1) * S],
                                                              scalar=W("b0p")[:, g:g + 1], in1=hT[p][:, g, :],
                                                              op0=add, op1=add)
                    last.then_inc(m0_read, 1)

            def rate_piece(b, name):
                p = b.par
                full = lambda: dve.wait_ge(m1_full, rate_no(b, name))
                base = RATE_LINKS * b.n
                if name == "ca":
                    full()
                    for g in range(G):
                        tt(k2b[:, g], M1[:, g * NCA:(g + 1) * NCA].unsqueeze(1).broadcast_to([P, HG, NCA]),
                           W("mask_h").unsqueeze(2).broadcast_to([P, HG, NCA]), mult)
                    tt(v2b[:, :], M1[0:H1 * NCA, S:2 * S], W("mask_v2", H1 * NCA), mult).then_inc(m1_read, 1)
                elif name[:2] == "cs":
                    full()
                    n = int(name[2])
                    nc.vector.tensor_reduce(cm[:, 2 * n:2 * n + 2], M1[:, :].rearrange("p (h s) -> p h s", h=2),
                                            AX.X, ALU.max, negate=True).then_inc(cm_ready, 1)
                elif name == "sc":
                    full()
                    s = M1[0:NC2, 0:H1 * NCA].rearrange("p (h t) -> p h t", h=H1)
                    nc.vector.reduce_max(m2[:, :], s, AX.X).then_inc(rate_chain, 1)
                    dve.wait_ge(rate_chain, base + 4)
                    tt(p2[:, :, :], s, m2[:, :].unsqueeze(2).broadcast_to([NC2, H1, NCA]), sub).then_inc(m1_read, 1)
                elif name in ("m0", "m1"):
                    g = int(name[1])
                    full()
                    wait(dve, mscr_done, 16 * (G * b.n + g))
                    at = base + (1, 7)[g]
                    m = M1[0:HG * QT, 0:P]
                    nc.vector.tensor_copy(msp[:, 0, :], m).then_inc(rate_chain, 1)
                    dve.wait_ge(rate_chain, at + 1)
                    tt(mr[:, :], m, msp[:, 0, :], sub).then_inc(m1_read, 1)
                    dve.wait_ge(m1_read, rate_no(b, name))
                    nc.vector.tensor_copy(msp[:, 1, :], mr[:, :]).then_inc(rate_chain, 1)
                    dve.wait_ge(rate_chain, at + 2)
                    tt(msp[:, 2, :], mr[:, :], msp[:, 1, :], sub).then_inc(msp_ready, 1)

            def group_max(b, g):
                n = HG * QT
                dve.wait_ge(sx_read, NMAX * b.n + (g + 1) * n * NCH)
                nc.vector.tensor_reduce(nm[:, g * n:(g + 1) * n], mx[:, g * n:(g + 1) * n, :], AX.X, ALU.max,
                                        negate=True).then_inc(rate_chain, 1)

            def sum_severity(b):
                dve.wait_ge(in_loaded[b.par], 48 * (b.half + 1))
                nc.vector.reduce_sum(sev[:, :], cT[b.par][:, 0:T0], AX.X).then_inc(sev_ready, 1)

            def step(prep, rate, att, fin):
                for k in range(UNITS):
                    if prep and PREP_SLOT.get(k - 1) in KEYS:
                        prep_piece(prep, PREP_SLOT[k - 1])
                    if prep and k in PREP_SLOT and PREP_SLOT[k] not in KEYS:
                        prep_piece(prep, PREP_SLOT[k])
                    if prep and k == 2:
                        dve.wait_ge(gz_exp, prep.n + 1)
                        nc.vector.tensor_scalar_add(gate[:, :], gate[:, :], 1.0).then_inc(prep_chain, 1)
                        dve.wait_ge(prep_chain, PREP_LINKS * prep.n + 3)
                        nc.vector.reciprocal(gate[:, :], gate[:, :]).then_inc(prep_chain, 1)
                    if prep and k == 10:
                        dve.wait_ge(e0_exp, prep.n + 1)
                        nc.vector.reduce_sum(d0[:, :, :], e0[:, :, :].rearrange("p t (g k) -> p t g k", k=T0), AX.X)\
                            .then_inc(prep_chain, 1)
                        dve.wait_ge(prep_chain, PREP_LINKS * prep.n + 8)
                        nc.vector.reciprocal(d0[:, :, :], d0[:, :, :]).then_inc(prep_chain, 1)
                        dve.wait_ge(prep_chain, PREP_LINKS * prep.n + 9)
                        for s in range(2):
                            for o, n in ((s * HA, HA), (2 * HA + s * HB, HB)):
                                nc.vector.tensor_scalar(d0[:, :, o:o + n], d0[:, :, o:o + n],
                                                        gate[:, s:s + 1], None, mult).then_inc(w0_ready, 1)
                    if prep and k == 46 and not (isinstance(prep.n, int) and prep.n == B - 1):
                        sum_severity(Batch(prep.i, prep.c + 1))
                    if rate and k == 24:
                        group_max(rate, 0)
                    if rate and k == 48:
                        group_max(rate, 1)
                    if rate and k in RATE_SLOT:
                        rate_piece(rate, RATE_SLOT[k])
                    if rate and k == 18:
                        dve.wait_ge(m1_read, rate_no(rate, "cs2"))
                        nc.vector.reciprocal(cm[:, :], cden[:, :]).then_inc(cden_ready, 1)
                    if rate and k == 43:
                        base = RATE_LINKS * rate.n + 4
                        dve.wait_ge(s2_exp, rate.n + 1)
                        dve.wait_ge(m1_read, rate_no(rate, "sc"))
                        nc.vector.reduce_sum(d2[:, :], p2[:, :, :], AX.X).then_inc(rate_chain, 1)
                        dve.wait_ge(rate_chain, base + 1)
                        nc.vector.reciprocal(d2[:, :], d2[:, :]).then_inc(rate_chain, 1)
                        dve.wait_ge(rate_chain, base + 2)
                        tt(p2[:, :, :], p2[:, :, :], d2[:, :].unsqueeze(2).broadcast_to([NC2, H1, NCA]), mult)\
                            .then_inc(p2_ready, 1)
                    for b, g, at in ((fin, 1, DEN1), (att, 0, DEN0)):
                        if b and k == at:
                            dve.wait_ge(fin_full, 3 * b.n + g + 1)
                            wait(dve, out_stored, 16 * b.n)
                            nc.vector.reciprocal(rb[:, g, :], M1[:, 0:S]).then_inc(fin_read, 1)
                    if fin and k == OUT:
                        dve.wait_ge(fin_full, 3 * fin.n + 3)
                        dve.wait_ge(res_ready, fin.n + 1)
                        tt(o1, M1[:, 0:QT * D],
                           res[fin.par][:, :, :].rearrange("p t d -> p (t d)"), add).then_inc(fin_read, 1)

                    if rate:
                        for h, t, c, n in chunks_of(k):
                            dve.wait_ge(sx_full, NMAX * rate.n + n + 1)
                            w = min(CH, NKEY - c * CH)
                            nc.vector.reduce_max(mx[:, h * QT + t, c:c + 1], SX[n % 2][:, 0:w], AX.X)\
                                .then_inc(sx_read, 1)

            sum_severity(Batch(0, 0))
            steps(dve, step)

        @block.gpsimd
        def _(pool):
            def tt(o, a, b, op):
                return nc.gpsimd.tensor_tensor(o, a, b, op)

            nc.gpsimd.memset(kspa[0:3, 0, :], 1.0).then_inc(consts, 1)
            for p in range(2):
                nc.gpsimd.memset(v[p][:, :, :, D1 + 1:PAD], 0.0)
                nc.gpsimd.memset(v[p][:, :, :, D1:D1 + 1], 1.0).then_inc(consts, 1)
            pool.wait_ge(w_loaded, 32)

            def split(b, name):
                at = KEYS.index(name)
                n = int(name[-1])
                if len(name) == 2:
                    rows, parts = SPLIT_A, [kspa[:, a, n * CH:(n + 1) * CH] for a in range(3)]
                else:
                    rows, parts = P, [kspb[:, a, n, :] for a in range(3)]
                pool.wait_ge(m0_read, prep_no(b, name))
                on_its_own(pool)
                nc.gpsimd.tensor_copy(parts[1], kr[0:rows, at % 2, :]).then_inc(split_chain, 1)
                pool.wait_ge(split_chain, len(KEYS) * b.n + at + 1)
                tt(parts[2], kr[0:rows, at % 2, :], parts[1], ALU.subtract).then_inc(ksp_ready, 1)

            def split_queries(b):
                at = 3 * b.n
                pool.wait_ge(m0_read, prep_no(b, "q1"))
                wait(pool, qscr_done, 32 * b.n)
                on_its_own(pool)
                nc.gpsimd.tensor_copy(qsp[:, 0, :], qs).then_inc(query_chain, 1)
                pool.wait_ge(query_chain, at + 1)
                tt(qr[:, :], qs, qsp[:, 0, :], ALU.subtract).then_inc(query_chain, 1)
                pool.wait_ge(query_chain, at + 2)
                on_its_own(pool)
                nc.gpsimd.tensor_copy(qsp[:, 1, :], qr[:, :]).then_inc(query_chain, 1)
                pool.wait_ge(query_chain, at + 3)
                tt(qsp[:, 2, :], qr[:, :], qsp[:, 1, :], ALU.subtract).then_inc(qsp_ready, 1)

            def store_maxima(b, g):
                pool.wait_ge(msp_ready, G * b.n + g + 1)
                wait(pool, m_loaded[g], 16 * b.n)
                on_its_own(pool)
                pool.dma_start(mscr[g].rearrange("a r q -> r a q"), msp[:, :, :]).then_inc(mscr_done, 16)

            def load_maxima(b, g):
                pool.wait_ge(mscr_done, 16 * (G * b.n + g + 1))
                on_its_own(pool)
                pool.dma_start(qa[b.par][KR:KR + 3, g * HG:(g + 1) * HG, :],
                               mscr[g].rearrange("a (h t) q -> a h (t q)", t=QT)).then_inc(m_loaded[g], 16)

            def normalise(b, g):
                pool.wait_ge(fin_read, 3 * b.n + g + 1)
                tt(us[:, g, :], us[:, g, :], rb[:, g, :], ALU.mult).then_inc(z_chain, 1)
                pool.wait_ge(z_chain, G * b.n + g + 1)
                tt(us[:, g, :], us[:, g, :], zc[b.par][:, g, :], ALU.add).then_inc(z1_ready, 1)

            def repeat_tokens(b):
                pool.wait_ge(in_loaded[b.par], 48 * (b.half + 1))
                wait(pool, m0_full, NPREP * (b.n - 1) + 1)
                on_its_own(pool)
                for s, t in enumerate((T0, 0)):
                    last = nc.gpsimd.tensor_copy(
                        tok0[:, s], cT[b.par][:, t:t + T0].unsqueeze(1).broadcast_to([C, 8, T0]))
                last.then_inc(tok0_ready, 1)

            def step(prep, rate, att, fin):
                for slot in range(UNITS + 1):
                    k = slot - 1
                    if att and slot == 0:
                        load_maxima(att, 1)
                    if prep and k == 42:
                        wait(pool, m1_full, NRATE * (prep.n - 1) + RATE.index("ca") + 1)
                        on_its_own(pool)
                        nc.gpsimd.tensor_copy(tok2[:, :, :], cT[prep.par][:, NKEY:NCTX].unsqueeze(1)
                                              .broadcast_to([C, H1, NCA])).then_inc(tok2_ready, 1)
                    if prep and k == 46 and not (isinstance(prep.n, int) and prep.n == B - 1):
                        repeat_tokens(Batch(prep.i, prep.c + 1))
                    if fin and k == DEN1 + 1:
                        normalise(fin, 1)
                    if prep and PREP_SLOT.get(k) in KEYS:
                        split(prep, PREP_SLOT[k])
                    if prep and k == 11:
                        pool.wait_ge(w0_ready, 4 * (prep.n + 1))
                        e = e0[:, :, :].rearrange("p t (g k) -> p t g k", k=T0)
                        tt(e, e, d0[:, :, :].unsqueeze(3).broadcast_to([P, QT, 2 * H0, T0]), ALU.mult)\
                            .then_inc(p0_ready, 1)
                    if prep and PREP_SLOT.get(k) == "q1":
                        split_queries(prep)
                    if rate and k == 16:
                        pool.wait_ge(m0_read, prep_no(rate, "hn"))
                        wait(pool, fin_read, 3 * (rate.n - 1))
                        for t in range(QT):
                            last = tt(res[rate.par][:, t, :].rearrange("p (h d) -> p h d", d=D1),
                                      hn[rate.par][:, t, :].rearrange("p (h d) -> p h d", d=PAD)[:, :, 0:D1],
                                      W("b1n").rearrange("p (h d) -> p h d", d=D1), ALU.add)
                        last.then_inc(res_ready, 1)
                    if rate and k == 5:
                        pool.wait_ge(m1_read, rate_no(rate, "caq"))
                        for g in range(G):
                            last = tt(caqb[:, g], caq[:, g, :].unsqueeze(1).broadcast_to([P, HG, NC2]),
                                      W("mask_h").unsqueeze(2).broadcast_to([P, HG, NC2]), ALU.mult)
                        last.then_inc(caqb_ready, 1)
                    if rate and k == 19:
                        pool.wait_ge(cden_ready, rate.n + 1)
                        tt(pc[:, :, :], pc[:, :, :], cm[:, :].unsqueeze(2).broadcast_to([P, CT, S]), ALU.mult)\
                            .then_inc(pc_ready, 1)
                    if rate and k == 29:
                        store_maxima(rate, 0)
                    if rate and k == 34:
                        load_maxima(rate, 0)
                    if att and k == DEN0 + 1:
                        normalise(att, 0)
                if rate:
                    store_maxima(rate, 1)

            repeat_tokens(Batch(0, 0))
            steps(pool, step)


def kernel(x, ctx_768, L0_xattn_w_q, L0_xattn_w_k, L0_xattn_w_v, L0_xattn_w_k_dis, L0_xattn_w_v_dis,
           L0_xattn_w_gate, L0_xattn_b_gate, L0_xattn_anat_gate_logit, L0_xattn_dis_gate_logit,
           L0_xattn_w_out, L0_xattn_b_out, L1_xattn_Wq, L1_xattn_Wk, L1_xattn_Wv, L1_xattn_Wq_ca,
           L1_xattn_Wk_ca, L1_xattn_Wv_ca, L1_xattn_Wout, L1_xattn_b_out):
    import concourse.bacc as bacc
    from concourse.bass_utils import run_bass_kernel_spmd

    def cols(a):
        a = np.asarray(a)
        out = np.zeros((*a.shape[:-1], G, HG, PAD), a.dtype)
        out[..., :D1] = a.reshape(*a.shape[:-1], G, HG, D1)
        return out.reshape(*a.shape[:-1], G * P)

    def rows(a):
        return cols(np.asarray(a).T).reshape(-1, G, P).transpose(2, 1, 0)

    def table(n, widths, at, items):
        out = np.zeros((n, sum(widths.values())), np.float32)
        for name, a in items.items():
            a = np.asarray(a)
            a = a.reshape(a.shape[0], -1)
            out[:a.shape[0], at[name][0]:at[name][0] + a.shape[1]] = a
        return out

    r = np.arange(P)
    same = lambda a, b: (a[:, None] == b[None, :])
    wo0 = cols(np.asarray(L0_xattn_w_out).T)
    wq1 = rows(L1_xattn_Wq)
    all_rows = lambda a: np.broadcast_to(np.asarray(a), (P, np.size(a)))
    items = dict(
        ident=np.eye(P), b0p=cols(L0_xattn_b_out).reshape(G, P).T,
        b1n=all_rows(L1_xattn_b_out),
        spread=(r[:, None] % PAD == D1) & same(r // PAD, r // PAD),
        mask_a=same(r // D0, np.arange(HA)), mask_b=same(r[:HB * D0] // D0, np.arange(HB)),
        mask_h=same(r // PAD, np.arange(HG)), mask_v=same(r // T0, np.arange(64) // D0),
        mask_v4=same(r % 64 // T0, np.arange(32) // D0),
        logits=np.stack([np.broadcast_to(np.asarray(a).reshape(()), (P,)) for a in (
            L0_xattn_b_gate, L0_xattn_anat_gate_logit, L0_xattn_dis_gate_logit)], 1),
        wq0=rows(np.asarray(L0_xattn_w_q).T), wo0a=wo0[:P], wo0b=wo0[P:],
        wq1=np.concatenate([wq1, np.zeros((P, G, 2 * SPLIT_A - D), np.float32)], 2),
        wqpp=cols(wq1), wo1=rows(L1_xattn_Wout),
        mask_v2=same(np.arange(H1 * NCA) // NCA, np.arange(G * P) // PAD))
    w128 = table(P, W128, O128, items)
    repeat = np.linspace(0, NC2 - 1, S).astype(np.int64)
    items = dict(
        wk0=np.asarray(L0_xattn_w_k).T, wkd0=np.asarray(L0_xattn_w_k_dis).T,
        wv0=np.asarray(L0_xattn_w_v).T, wvd0=np.asarray(L0_xattn_w_v_dis).T,
        wg=np.asarray(L0_xattn_w_gate).T, repeat=same(np.arange(NC2), repeat),
        wk1=L1_xattn_Wk, wv1=L1_xattn_Wv, wkca=cols(L1_xattn_Wk_ca), wvca=cols(L1_xattn_Wv_ca),
        wqca=cols(L1_xattn_Wq_ca))
    w96 = table(C, W96, O96, items)
    xp = cols(x)
    c = np.asarray(ctx_768)
    arrays = {
        "x_t": xp.reshape(B, S, G, P).transpose(0, 3, 2, 1),
        "ctx_t": c.transpose(0, 2, 1), "ca_n": c[:, NKEY:], "w128": w128, "w96": w96,
    }
    arrays = {n: np.ascontiguousarray(a) for n, a in arrays.items()}
    nc = bacc.Bacc("TRN2", target_bir_lowering=False, num_devices=1)
    aps = [nc.dram_tensor(n, a.shape, mybir.dt.from_np(a.dtype), kind="ExternalInput").ap()
           for n, a in arrays.items()]
    out = nc.dram_tensor("out", (B, S, D), mybir.dt.float32, kind="ExternalOutput").ap()
    program(nc, *aps, out)
    return run_bass_kernel_spmd(nc, [arrays], core_ids=[0]).results[0]["out"]
```

```python
import numpy as np

import concourse.bass as bass
from concourse import mybir
from contextlib import ExitStack

B, S, D, C, NKEY, NCA = 8, 256, 160, 96, 1597, 4
NCTX = NKEY + NCA
P = 128
QT = S // P
H0, D0, T0 = 20, 8, 16
HA = P // D0
HB = H0 - HA
H1, D1 = 8, 20
G, HG = 2, 4
PAD = 32
KT = -(-NKEY // P)
LAST = NKEY - (KT - 1) * P
CH = 400
NCH = 4
KW = CH * NCH
NC2 = 96
CT = H1 * NC2 // P
HALF = 2
UNITS = G * KT * (HG // HALF)
ST = 2
NX = 3
NP = 4
PARTS_K = (0, 0, 0, 1, 1, 2)
PARTS_Q = (0, 1, 2, 0, 1, 0)
TERMS = len(PARTS_K)
KR = TERMS * D1
SPLIT_A = 6 * D1
SPLIT_B = D - SPLIT_A

EARLY = dict(ident=128, mask_a=HA, mask_b=HB, mask_h=HG, mask_v=64, mask_v4=32, b0p=G, b1n=D,
             logits=3, wq0=G * D, mask_v2=G * P)
W128 = dict(**EARLY, spread=128, wo0a=G * P, wo0b=G * P, wq1=G * 2 * SPLIT_A, wqpp=G * G * P,
            wo1=G * D)
W96 = dict(wk0=D, wkd0=D, wv0=D, wvd0=D, wg=1, repeat=S, wk1=SPLIT_A + 64, wv1=D, wkca=G * P,
           wvca=G * P, wqca=G * P)


def offsets(table):
    at, out = 0, {}
    for name, n in table.items():
        out[name] = (at, at + n)
        at += n
    return out, at


O128, N128 = offsets(W128)
NEARLY = offsets(EARLY)[1]
O96, N96 = offsets(W96)

PREP_SLOT = {0: "small", 2: "q0", 4: "s0", 6: "s1", 8: "s2", 10: "k0", 13: "k1", 16: "t0",
             18: "t1", 20: "t2", 22: "z", 24: "k2", 26: "h", 28: "q1", 30: "k3", 32: "kb0",
             34: "kb1", 39: "hn"}
KEYS = ["k0", "k1", "k2", "k3", "kb0", "kb1"]
PREP = [PREP_SLOT[n] for n in sorted(PREP_SLOT) if PREP_SLOT[n] not in KEYS]
FIRST_SLOT = {n: name for n, name in PREP_SLOT.items() if name not in KEYS}
FIRST_SLOT.update(zip((1, 3, 5, 13, 17, 21), KEYS))
RATE_SLOT = {1: "ca", 3: "caq", 7: "v0", 11: "cs0", 13: "cs1", 15: "cs2", 17: "v1", 20: "v2",
             22: "v3", 24: "ct0", 26: "ct1", 28: "m0", 30: "ct2", 32: "v4", 34: "c1", 36: "c2",
             41: "sc", 45: "pe", 47: "zc", 51: "m1"}
RATE = [RATE_SLOT[n] for n in sorted(RATE_SLOT)]
DEN1, OUT, DEN0 = 5, 9, 38
MAX_SLOTS = 47
NRATE, NPREP = len(RATE), len(PREP)
NMAX = H1 * QT * NCH
PREP_LINKS = 10
RATE_LINKS = 9
KSTORES = 7


class Batch:

    def __init__(self, i, c):
        self.i, self.c, self.par = i, c, c % 2

    @property
    def n(self):
        return 2 * self.i + self.c

    @property
    def half(self):
        return self.i + self.c // 2

    @property
    def first(self):
        return isinstance(self.n, int) and self.n == 0

    @property
    def second(self):
        return isinstance(self.n, int) and self.n == 1

    @property
    def slots(self):
        return FIRST_SLOT if self.first else PREP_SLOT


def wait(eng, sem, value):
    if not (isinstance(value, int) and value <= 0):
        eng.wait_ge(sem, value)


def steps(eng, step):
    one = lambda c: Batch(0, c)
    step(one(0), None, None, None)
    step(one(1), one(0), None, None)
    step(one(2), one(1), one(0), None)
    with eng.Fori(0, 2) as i:
        for c in (1, 2):
            step(Batch(i, c + 2), Batch(i, c + 1), Batch(i, c), Batch(i, c - 1))
    step(one(7), one(6), one(5), one(4))
    step(None, one(7), one(6), one(5))
    step(None, None, one(7), one(6))
    step(None, None, None, one(7))


def program(nc, x_t, ctx_t, ca_n, w128, w96, out):
    fp32, bf16 = mybir.dt.float32, mybir.dt.bfloat16
    ALU, ACT, AX = mybir.AluOpType, mybir.ActivationFunctionType, mybir.AxisListType
    SC0 = 1.0 / float(np.sqrt(D0))
    SC1 = float(D1) ** -0.5

    ctx = ExitStack()
    with ctx:
        def sb(name, shape, dt=fp32):
            return ctx.enter_context(nc.sbuf_tensor(name, shape, dt))

        def sem(name):
            return ctx.enter_context(nc.semaphore(name))

        wp = sb("wp", [P, N128])
        wc = sb("wc", [C, N96])

        def W(name, rows=P):
            return wp[0:rows, O128[name][0]:O128[name][1]]

        def Wc(name, rows=C):
            return wc[0:rows, O96[name][0]:O96[name][1]]

        cT = [sb(f"cT{p}", [C, NCTX]) for p in range(2)]
        can = [sb(f"can{p}", [NCA, C]) for p in range(2)]
        sev = sb("sev", [C, 1])
        tok0 = sb("tok0", [C, 2, 8, T0])
        tok2 = sb("tok2", [C, H1, NCA])
        gz = sb("gz", [P, 2])
        gate = sb("gate", [P, 2])
        kb0a = sb("kb0a", [P, 2, HA, T0])
        kb0b = sb("kb0b", [HB * D0, 2, HB, T0])
        vb0 = sb("vb0", [P, 4, 64])
        vb4 = sb("vb4", [P, 32])
        q0a = sb("q0a", [P, S])
        q0b = sb("q0b", [HB * D0, S])
        e0 = sb("e0", [P, QT, 2 * H0 * T0])
        m0x = sb("m0x", [P, QT, 2 * H0])
        d0 = sb("d0", [P, QT, 2 * H0])
        pT0 = sb("pT0", [P, 5, S])
        z0a = sb("z0a", [P, S])
        z0b = sb("z0b", [HB * D0, S])
        hT = [sb(f"hT{p}", [P, G, S]) for p in range(2)]
        hn = [sb(f"hn{p}", [P, QT, G * P]) for p in range(2)]
        res = [sb(f"res{p}", [P, QT, D]) for p in range(2)]
        qs = e0[0:SPLIT_A, 0, 0:2 * S]
        qsp = sb("qsp", [SPLIT_A, 3, 2 * S], bf16)
        kr = sb("kr", [P, 2, CH])
        qr = sb("qr", [SPLIT_A, 2 * S])
        kspa = sb("kspa", [SPLIT_A, 3, KW], bf16)
        kspb = sb("kspb", [P, 3, 2, CH], bf16)
        ka = [sb(f"ka{p}", [KR + 3, H1, KW], bf16) for p in range(2)]
        qa = [sb(f"qa{p}", [KR + 3, H1, S], bf16) for p in range(2)]
        mx = sb("mx", [P, H1 * QT, NCH])
        nm = sb("nm", [P, H1 * QT])
        mr = sb("mr", [HG * QT, P])
        msp = sb("msp", [HG * QT, 3, P], bf16)
        v = [sb(f"v{p}", [P, KT, H1, PAD]) for p in range(2)]
        pr = sb("pr", [P, NP, HALF * S])
        k2b = sb("k2b", [P, G, HG, NCA])
        v2b = sb("v2b", [H1 * NCA, G * P])
        caq = sb("caq", [P, G, NC2])
        caqb = sb("caqb", [P, G, HG, NC2])
        cm = sb("cm", [P, CT])
        cden = sb("cden", [P, CT])
        pc = sb("pc", [P, CT, S])
        pcT = sb("pcT", [P, QT, CT * P])
        c1T = sb("c1T", [P, G, NC2])
        c2T = sb("c2T", [P, G, NC2])
        p2 = sb("p2", [NC2, H1, NCA])
        m2 = sb("m2", [NC2, H1])
        d2 = sb("d2", [NC2, H1])
        p2e = sb("p2e", [H1 * NCA, S])
        zc = [sb(f"zc{p}", [P, G, S]) for p in range(2)]
        us = sb("us", [P, G, S])
        rb = sb("rb", [P, G, S])
        o1 = rb[:, :, :].rearrange("p g s -> p (g s)")[:, 0:QT * D]

        bank = [ctx.enter_context(nc.psum_tensor(f"bank{n}", [P, 512], fp32)) for n in range(8)]
        U, SX, M0, M1 = bank[3], [bank[2], bank[4], bank[5]], bank[6], bank[7]

        FREE = [bank[0], bank[1], U]

        kscr = nc.dram_tensor("kscr", (2, 3, D, KW), bf16).ap()
        qscr = nc.dram_tensor("qscr", (2, 3, D, S), bf16).ap()
        mscr = nc.dram_tensor("mscr", (G, 3, HG * QT, P), bf16).ap()

        w_loaded = sem("w_loaded")
        late_loaded = sem("late_loaded")
        in_loaded = [sem(f"in_loaded{p}") for p in range(2)]
        ones_loaded = sem("ones_loaded")
        consts = sem("consts")
        m0_full, m0_read = sem("m0_full"), sem("m0_read")
        keys_full, keys_read = sem("keys_full"), sem("keys_read")
        m1_full, m1_read = sem("m1_full"), sem("m1_read")
        fin_full, fin_read = sem("fin_full"), sem("fin_read")
        sev_ready = sem("sev_ready")
        gz_ready, gz_exp = sem("gz_ready"), sem("gz_exp")
        prep_chain = sem("prep_chain")
        rate_chain = sem("rate_chain")
        split_chain = sem("split_chain")
        query_chain = sem("query_chain")
        z_chain = sem("z_chain")
        e0_exp, w0_ready, p0_ready = sem("e0_exp"), sem("w0_ready"), sem("p0_ready")
        tok0_ready, tok2_ready = sem("tok0_ready"), sem("tok2_ready")
        k1_ready = sem("k1_ready")
        ksp_ready, qsp_ready = sem("ksp_ready"), sem("qsp_ready")
        kscr_done, qscr_done = sem("kscr_done"), sem("qscr_done")
        kq_loaded = [[sem(f"kq_loaded{p}{g}") for g in range(G)] for p in range(2)]
        sx_full, sx_read = sem("sx_full"), sem("sx_read")
        msp_ready = sem("msp_ready")
        mscr_done = sem("mscr_done")
        m_loaded = [sem(f"m_loaded{g}") for g in range(G)]
        st_full, exp_done, pv_done = sem("st_full"), sem("exp_done"), sem("pv_done")
        caqb_ready, cm_ready = sem("caqb_ready"), sem("cm_ready")
        cden_ready, pc_ready = sem("cden_ready"), sem("pc_ready")
        s2_exp, p2_ready = sem("s2_exp"), sem("p2_ready")
        res_ready = sem("res_ready")
        u_read, z1_ready = sem("u_read"), sem("z1_ready")
        out_stored = sem("out_stored")
        passed = sem("passed")

        prep_no = lambda b, name: NPREP * b.n + PREP.index(name) + 1
        keys_no = lambda b, name: len(KEYS) * b.n + KEYS.index(name) + 1
        rate_no = lambda b, name: NRATE * b.n + RATE.index(name) + 1

        def chunks_of(k):
            return [(n // (QT * NCH), n // NCH % QT, n % NCH, n)
                    for n in range(NMAX) if n * MAX_SLOTS // NMAX == k]

        def unit(k):
            return k // (KT * 2), k // 2 % KT, k % 2

        def keys_bank(b, name):
            at = KEYS.index(name)
            return bank[at] if b.first else FREE[at % len(FREE)] if b.second else M0

        def last_use(n, total, banks):
            return n - banks if n >= banks else next(m for m in range(-1, -banks - 1, -1)
                                                     if (total + m) % banks == n)

        def on_its_own(eng):
            eng.sem_inc(passed, 1)

        def split_queries(eng, unit, b):
            at = 2 * b.n
            eng.wait_ge(m0_read, prep_no(b, "q1"))
            unit.tensor_tensor(qr[:, :], qs, qsp[:, 0, :], ALU.subtract).then_inc(query_chain, 1)
            eng.wait_ge(query_chain, at + 1)
            if not b.first:
                on_its_own(eng)
            unit.tensor_copy(qsp[:, 1, :], qr[:, :]).then_inc(query_chain, 1)
            eng.wait_ge(query_chain, at + 2)
            unit.tensor_tensor(qsp[:, 2, :], qr[:, :], qsp[:, 1, :], ALU.subtract).then_inc(qsp_ready, 1)

        block = ctx.enter_context(nc.Block())

        def load_inputs(eng, b):
            p = b.par
            eng.dma_start(cT[p][:, :], ctx_t[bass.ds(b.n, 1)].rearrange("a c n -> (a c) n"))\
              .then_inc(in_loaded[p], 16)
            eng.dma_start(hT[p][:, :, :], x_t[bass.ds(b.n, 1)].rearrange("a p g s -> (a p) g s"))\
              .then_inc(in_loaded[p], 16)
            eng.dma_start(can[p][:, :], ca_n[bass.ds(b.n, 1)].rearrange("a t c -> (a t) c"))\
              .then_inc(in_loaded[p], 16)

        def load_parts(eng, b, g, stack, scr, parts):
            wait(eng, st_full, UNITS * (b.n - 2) + (g + 1) * (UNITS // G))
            on_its_own(eng)
            for t in range(TERMS):
                src = scr[b.par, parts[t]].rearrange("(g h d) n -> g d h n", g=G, h=HG)[g]
                eng.dma_start(stack[b.par][t * D1:(t + 1) * D1, g * HG:(g + 1) * HG, :], src)\
                  .then_inc(kq_loaded[b.par][g], 16)

        def send_queries(eng, b):
            eng.wait_ge(qsp_ready, b.n + 1)
            on_its_own(eng)
            dst = qscr[b.par].rearrange("a r n -> r a n")
            eng.dma_start(dst[0:SPLIT_A], qsp[:, :, 0:S]).then_inc(qscr_done, 16)
            eng.dma_start(dst[SPLIT_A:D], qsp[0:SPLIT_B, :, S:2 * S]).then_inc(qscr_done, 16)
            eng.wait_ge(qscr_done, 32 * (b.n + 1))
            on_its_own(eng)

        @block.sync
        def _(sp):
            sp.dma_start(wc[:, :], w96).then_inc(w_loaded, 16)
            load_inputs(sp, Batch(0, 0))
            sp.wait_ge(consts, 1)
            for p in range(2):
                sp.dma_start(ka[p][KR:KR + 3, :, :], kspa[0:3, 0:1, :].broadcast_to([3, H1, KW]))\
                  .then_inc(ones_loaded, 16)

            def send_keys(b):
                sp.wait_ge(ksp_ready, len(KEYS) * b.n + NCH)
                on_its_own(sp)
                sp.dma_start(kscr[b.par].rearrange("a r n -> r a n")[0:SPLIT_A], kspa[:, :, :])\
                  .then_inc(kscr_done, 16)
                sp.wait_ge(ksp_ready, len(KEYS) * (b.n + 1))
                on_its_own(sp)
                for u in range(2):
                    for a in range(3):
                        dst = kscr[b.par, a, SPLIT_A:D].rearrange("r (c u n) -> u r c n", c=2, u=2)[u]
                        sp.dma_start(dst, kspb[64 * u:64 * u + SPLIT_B, a, :, :]).then_inc(kscr_done, 16)
                sp.wait_ge(kscr_done, 16 * KSTORES * (b.n + 1))
                on_its_own(sp)

            def step(prep, rate, att, fin):
                if rate and not rate.first:
                    load_parts(sp, rate, 1, qa, qscr, PARTS_Q)
                    load_parts(sp, rate, 1, ka, kscr, PARTS_K)
                if fin:
                    sp.wait_ge(fin_read, 3 * (fin.n + 1))
                    on_its_own(sp)
                    sp.dma_start(out[bass.ds(fin.n, 1)].rearrange("a (t q) d -> q (a t) d", q=P),
                                 o1.rearrange("p (t d) -> p t d", t=QT)).then_inc(out_stored, 16)
                if prep and prep.first:
                    send_keys(prep)
                    for g in range(G):
                        load_parts(sp, prep, g, ka, kscr, PARTS_K)
                elif prep:
                    wait(sp, kq_loaded[prep.par][1], 16 * 2 * TERMS * prep.half)
                    on_its_own(sp)
                    send_queries(sp, prep)
                    load_parts(sp, prep, 0, qa, qscr, PARTS_Q)
                    send_keys(prep)
                    load_parts(sp, prep, 0, ka, kscr, PARTS_K)

            load_inputs(sp, Batch(0, 1))
            steps(sp, step)
            sp.wait_ge(out_stored, 16 * B)

        @block.tensor
        def _(pe):
            def mm(o, lhs, rhs, start=True, stop=True):
                return nc.tensor.matmul(o, lhs, rhs, start=start, stop=stop)

            pe.wait_ge(w_loaded, 32)
            pe.wait_ge(consts, 3)
            pe.wait_ge(ones_loaded, 32)
            tok = [slice(T0, 2 * T0), slice(0, T0)]
            tail = slice(NKEY, NCTX)

            def prep_piece(b, at, name):
                p = b.par
                before = [x for k, x in b.slots.items() if k < at]
                if b.second and name in KEYS:
                    pe.wait_ge(keys_read, keys_no(b, name) - len(FREE))
                elif not (b.first and name in KEYS):
                    wait(pe, m0_read, NPREP * b.n + sum(x not in KEYS for x in before))
                    if not (b.first or b.second):
                        wait(pe, keys_read, len(KEYS) * b.n + sum(x in KEYS for x in before))
                wk = [Wc("wk0"), Wc("wkd0")]
                wv = [Wc("wv0"), Wc("wvd0")]
                if name == "small":
                    pe.wait_ge(in_loaded[p], 48 * (b.half + 1))
                    pe.wait_ge(tok0_ready, b.n + 1)
                    for s in range(2):
                        r8 = tok0[:, s, :, :].rearrange("p h k -> p (h k)")
                        t = cT[p][:, tok[s]]
                        mm(M0[:, s * T0:(s + 1) * T0], wk[s][:, 0:P], t)
                        mm(M0[0:HB * D0, 32 + s * T0:32 + (s + 1) * T0], wk[s][:, P:D], t)
                        for u in range(2):
                            c = 2 * s + u
                            mm(M0[:, 64 + 64 * c:128 + 64 * c],
                               r8, wv[s][:, 64 * u:64 * u + 64])
                        mm(M0[64 * s:64 * s + 64, 320:352],
                           r8[:, 0:HB * T0], wv[s][:, P:D])
                    pe.wait_ge(sev_ready, b.n + 1)
                    last = mm(M0[:, 352:353], Wc("wg").broadcast_to([C, P]), sev[:, :])
                elif name == "q0":
                    for cols, o in ((slice(0, P), M0[:, 0:S]), (slice(P, D), M0[0:HB * D0, S:2 * S])):
                        for g in range(G):
                            last = mm(o, W("wq0").rearrange("p (g d) -> p g d", g=G)[:, g, cols],
                                      hT[p][:, g, :], g == 0, g == G - 1)
                elif name in ("k0", "k1", "k2", "k3"):
                    c = int(name[1])
                    mm(keys_bank(b, name)[0:SPLIT_A, 0:CH], Wc("wk1")[:, 0:SPLIT_A],
                       cT[p][:, c * CH:(c + 1) * CH]).then_inc(keys_full, 1)
                    return
                elif name in ("kb0", "kb1"):
                    for u in range(2):
                        c = 2 * int(name[2]) + u
                        last = mm(keys_bank(b, name)[64 * u:64 * u + 64, 0:CH],
                                  Wc("wk1")[:, SPLIT_A:SPLIT_A + 64], cT[p][:, c * CH:(c + 1) * CH])
                    last.then_inc(keys_full, 1)
                    return
                elif name in ("s0", "s1"):
                    t = int(name[1])
                    last = mm(M0[:, :], q0a[:, t * P:(t + 1) * P], kb0a[:, :, :, :].rearrange("p s h k -> p (s h k)"))
                elif name == "s2":
                    for t in range(QT):
                        last = mm(M0[:, t * P:(t + 1) * P], q0b[:, t * P:(t + 1) * P],
                                  kb0b[:, :, :, :].rearrange("p s h k -> p (s h k)"))
                elif name in ("t0", "t1", "t2"):
                    pe.wait_ge(p0_ready, b.n + 1)
                    for c in range(2 * int(name[1]), min(2 * int(name[1]) + 2, 5)):
                        for t in range(QT):
                            o = (c % 2) * S + t * P
                            last = nc.tensor.transpose(M0[:, o:o + P], e0[:, t, c * P:(c + 1) * P], W("ident"))
                elif name == "z":
                    for u in range(2):
                        for s in range(2):
                            mm(M0[64 * u:64 * u + 64, 0:S], vb0[:, 2 * s + u, :], pT0[:, 2 * s + u, :],
                               s == 0, s == 1)
                    last = mm(M0[0:32, S:2 * S], vb4[:, :], pT0[:, 4, :])
                elif name == "h":
                    if b.first:
                        pe.wait_ge(late_loaded, 16)
                    for g in range(G):
                        o = M0[:, g * S:(g + 1) * S]
                        mm(o, W("wo0a")[:, g * P:(g + 1) * P], z0a[:, :], True, False)
                        last = mm(o, W("wo0b", 32)[:, g * P:(g + 1) * P], z0b[:, :], False, True)
                elif name == "hn":
                    for t in range(QT):
                        for g in range(G):
                            last = nc.tensor.transpose(M0[:, (t * G + g) * P:(t * G + g + 1) * P],
                                                       hT[p][:, g, t * P:(t + 1) * P], W("ident"))
                elif name == "q1":
                    w = W("wq1").rearrange("p (g d) -> p g d", g=G)
                    for u in range(2):
                        for g in range(G):
                            last = mm(M0[0:SPLIT_A, u * S:(u + 1) * S], w[:, g, u * SPLIT_A:(u + 1) * SPLIT_A],
                                      hT[p][:, g, :], g == 0, g == G - 1)
                last.then_inc(m0_full, 1)

            def rate_piece(b, name):
                p, at = b.par, RATE.index(name)
                wait(pe, m1_read, NRATE * b.n + at)
                if name[0] == "v":
                    for t in range(3 * int(name[1]), min(3 * int(name[1]) + 3, KT)):
                        rows = P if t < KT - 1 else LAST
                        o = (t % 3) * D
                        last = mm(M1[0:rows, o:o + D], cT[p][:, t * P:t * P + rows], Wc("wv1"))
                elif name == "ca":
                    for g in range(G):
                        mm(M1[:, g * NCA:(g + 1) * NCA], Wc("wkca")[:, g * P:(g + 1) * P], cT[p][:, tail])
                    pe.wait_ge(tok2_ready, b.n + 1)
                    last = mm(M1[0:H1 * NCA, S:2 * S], tok2[:, :, :].rearrange("p h k -> p (h k)"),
                              Wc("wvca"))
                elif name == "caq":
                    for g in range(G):
                        last = mm(M1[:, g * NC2:(g + 1) * NC2], Wc("wqca", NCA)[:, g * P:(g + 1) * P],
                                  can[p][:, :])
                elif name[:2] == "cs":
                    pe.wait_ge(caqb_ready, b.n + 1)
                    for u in range(2):
                        g, m = divmod(2 * int(name[2]) + u, CT // G)
                        last = mm(M1[:, u * S:(u + 1) * S],
                                  caqb[:, g].rearrange("p h c -> p (h c)")[:, m * P:(m + 1) * P],
                                  hT[p][:, g, :])
                elif name[:2] == "ct":
                    pe.wait_ge(pc_ready, b.n + 1)
                    for n in range(4):
                        m, t = 2 * int(name[2]) + n // 2, n % 2
                        last = nc.tensor.transpose(M1[:, n * P:(n + 1) * P], pc[:, m, t * P:(t + 1) * P],
                                                   W("ident"))
                elif name == "c1":
                    for g in range(G):
                        for t in range(QT):
                            for j in range(HG):
                                last = mm(M1[PAD * j:PAD * (j + 1), g * NC2:(g + 1) * NC2],
                                          hn[p][:, t, g * P + PAD * j:g * P + PAD * (j + 1)],
                                          pcT[:, t, (g * HG + j) * NC2:(g * HG + j + 1) * NC2],
                                          t == 0, t == QT - 1)
                elif name == "c2":
                    w = W("wqpp").rearrange("p (a g d) -> p a g d", a=G, g=G)
                    for g in range(G):
                        for a in range(G):
                            last = mm(M1[:, g * NC2:(g + 1) * NC2], w[:, a, g, :], c1T[:, a, :],
                                      a == 0, a == G - 1)
                elif name == "sc":
                    for g in range(G):
                        last = mm(M1[0:NC2, g * HG * NCA:(g + 1) * HG * NCA], c2T[:, g, :],
                                  k2b[:, g, :, :].rearrange("p h t -> p (h t)"))
                elif name == "pe":
                    pe.wait_ge(p2_ready, b.n + 1)
                    last = mm(M1[0:H1 * NCA, 0:S], p2[:, :, :].rearrange("p h t -> p (h t)"),
                              Wc("repeat", NC2))
                elif name == "zc":
                    for g in range(G):
                        last = mm(M1[:, g * S:(g + 1) * S], v2b[:, g * P:(g + 1) * P], p2e[:, :])
                else:
                    g = int(name[1])
                    pe.wait_ge(rate_chain, RATE_LINKS * b.n + (1, 7)[g])
                    n = HG * QT
                    last = nc.tensor.transpose(M1[0:n, 0:P], nm[:, g * n:(g + 1) * n], W("ident"))
                last.then_inc(m1_full, 1)

            def max_scores(b, k):
                p = b.par
                for h, t, c, n in chunks_of(k):
                    if n % (HG * QT * NCH) == 0:
                        pe.wait_ge(kq_loaded[p][h // HG], 16 * 2 * TERMS * (b.half + 1))
                    wait(pe, sx_read, NMAX * b.n + last_use(n, NMAX, NX) + 1)
                    w = min(CH, NKEY - c * CH)
                    mm(SX[n % NX][:, 0:w], qa[p][0:KR, h, t * P:(t + 1) * P], ka[p][0:KR, h, c * CH:c * CH + w])\
                        .then_inc(sx_full, 1)

            def scores(b, k):
                p = b.par
                g, t, u = unit(k)
                if k % (UNITS // G) == 0:
                    pe.wait_ge(m_loaded[g], 16 * (b.n + 1))
                    if b.first and g == 0:
                        pe.wait_ge(keys_read, 2 * len(KEYS))
                wait(pe, exp_done, UNITS * b.n + last_use(k, UNITS, ST) + 1)
                rows = P if t < KT - 1 else LAST
                for j in range(HALF):
                    h = g * HG + HALF * u + j
                    last = mm(bank[k % ST][0:rows, j * S:(j + 1) * S], ka[p][:, h, t * P:t * P + rows],
                              qa[p][:, h, :])
                last.then_inc(st_full, 1)

            def values(b, k):
                p = b.par
                g, t, u = unit(k)
                if k % (UNITS // G) == 0:
                    if g == 0:
                        pe.wait_ge(m1_read, rate_no(b, "v4"))
                    wait(pe, u_read, G * b.n + g)
                pe.wait_ge(exp_done, UNITS * b.n + k + 1)
                rows = P if t < KT - 1 else LAST
                if rows < P:
                    on_its_own(pe)
                for j in range(HALF):
                    q = HALF * u + j
                    last = mm(U[PAD * q:PAD * (q + 1), g * S:(g + 1) * S], v[p][0:rows, t, g * HG + q, :],
                              pr[0:rows, k % NP, j * S:(j + 1) * S], t == 0, t == KT - 1)
                last.then_inc(pv_done, 1)

            def denominators(b, g):
                pe.wait_ge(u_read, G * b.n + g + 1)
                wait(pe, fin_read, 3 * b.n + g)
                mm(M1[:, 0:S], W("spread"), us[:, g, :]).then_inc(fin_full, 1)

            def project(b):
                pe.wait_ge(z1_ready, G * (b.n + 1))
                pe.wait_ge(fin_read, 3 * b.n + 2)
                for t in range(QT):
                    for g in range(G):
                        last = mm(M1[:, t * D:(t + 1) * D], us[:, g, t * P:(t + 1) * P],
                                  W("wo1").rearrange("p (g d) -> p g d", g=G)[:, g, :], g == 0, g == G - 1)
                last.then_inc(fin_full, 1)

            def step(prep, rate, att, fin):
                for k in range(UNITS):
                    if att:
                        scores(att, k)
                        if k % 2 and k > 2:
                            values(att, k - 3)
                            values(att, k - 2)
                    if prep and k in prep.slots:
                        prep_piece(prep, k, prep.slots[k])
                    if rate and k in RATE_SLOT:
                        if fin and k > DEN1:
                            pe.wait_ge(fin_read, 3 * fin.n + (2 if k < OUT else 3))
                        if att and k > DEN0:
                            pe.wait_ge(fin_read, 3 * att.n + 1)
                        rate_piece(rate, RATE_SLOT[k])
                    if fin and k in (DEN1, OUT) or att and k == DEN0:
                        before = RATE[sum(n < k for n in RATE_SLOT) - 1]
                        pe.wait_ge(m1_read, rate_no(rate, before) if rate else NRATE * B)
                    if fin and k == DEN1:
                        denominators(fin, 1)
                    if fin and k == OUT:
                        project(fin)
                    if att and k == DEN0:
                        denominators(att, 0)
                    if rate:
                        max_scores(rate, k)
                if att:
                    values(att, UNITS - 2)
                    values(att, UNITS - 1)

            steps(pe, step)

        @block.scalar
        def _(act):
            def f(o, i, func=ACT.Copy, **kw):
                return nc.scalar.activation(o, i, func, **kw)

            def prep_piece(b, name):
                if name in ("k0", "k1", "k2", "k3", "kb0", "kb1"):
                    act.wait_ge(keys_full, keys_no(b, name))
                    wait(act, kscr_done, 16 * KSTORES * b.n)
                    n = int(name[-1])
                    if len(name) == 2:
                        f(kspa[:, 0, n * CH:(n + 1) * CH], keys_bank(b, name)[0:SPLIT_A, 0:CH]).then_inc(k1_ready, 1)
                    else:
                        f(kspb[:, 0, n, :], keys_bank(b, name)[:, 0:CH]).then_inc(k1_ready, 1)
                elif name == "q0":
                    act.wait_ge(m0_full, prep_no(b, name))
                    f(q0a[:, :], M0[:, 0:S], scale=SC0)
                    f(q0b[:, :], M0[0:HB * D0, S:2 * S], scale=SC0).then_inc(m0_read, 1)
                elif name in ("t0", "t1", "t2"):
                    act.wait_ge(m0_full, prep_no(b, name))
                    n = int(name[1])
                    w = 1 if n == 2 else 2
                    f(pT0[:, 2 * n:2 * n + w, :].rearrange("p a s -> p (a s)"), M0[:, 0:w * S]).then_inc(m0_read, 1)
                elif name == "z":
                    act.wait_ge(m0_full, prep_no(b, name))
                    f(z0a[:, :], M0[:, 0:S])
                    f(z0b[:, :], M0[0:32, S:2 * S]).then_inc(m0_read, 1)
                elif name == "hn":
                    act.wait_ge(m0_full, prep_no(b, name))
                    f(hn[b.par][:, :, :].rearrange("p t d -> p (t d)"), M0[:, :]).then_inc(m0_read, 1)
                elif name == "q1":
                    act.wait_ge(m0_full, prep_no(b, name))
                    wait(act, qscr_done, 32 * b.n)
                    f(qs, M0[0:SPLIT_A, :], scale=SC1)
                    f(qsp[:, 0, :], M0[0:SPLIT_A, :], scale=SC1).then_inc(m0_read, 1)

            def rate_piece(b, name):
                p = b.par
                if name[0] == "v":
                    act.wait_ge(m1_full, rate_no(b, name))
                    wait(act, pv_done, UNITS * (b.n - 1))
                    n = int(name[1])
                    t0, t1 = 3 * n, min(3 * n + 3, KT)
                    rows = P if t1 < KT else LAST
                    f(v[p][0:rows, t0:t1, :, 0:D1],
                      M1[0:rows, 0:(t1 - t0) * D].rearrange("p (t h d) -> p t h d", h=H1, d=D1))\
                        .then_inc(m1_read, 1)
                elif name == "caq":
                    act.wait_ge(m1_full, rate_no(b, name))
                    wait(act, caqb_ready, b.n)
                    f(caq[:, :, :].rearrange("p g c -> p (g c)"), M1[:, 0:G * NC2], scale=SC1).then_inc(m1_read, 1)
                elif name[:2] == "cs":
                    n = int(name[2])
                    act.wait_ge(cm_ready, CT // 2 * b.n + n + 1)
                    for u in range(2):
                        h = 2 * n + u
                        last = f(pc[:, h, :], M1[:, u * S:(u + 1) * S], ACT.Exp, bias=cm[:, h:h + 1],
                                 accum_out=cden[:, h:h + 1])
                    last.then_inc(m1_read, 1)
                elif name[:2] == "ct":
                    act.wait_ge(m1_full, rate_no(b, name))
                    n = int(name[2])
                    f(pcT[:, :, 2 * n * P:(2 * n + 2) * P].rearrange("p t (u c) -> p u t c", u=2),
                      M1[:, :].rearrange("p (u t c) -> p u t c", u=2, t=QT)).then_inc(m1_read, 1)
                elif name == "c1":
                    act.wait_ge(m1_full, rate_no(b, name))
                    f(c1T[:, :, :].rearrange("p g c -> p (g c)"), M1[:, 0:G * NC2]).then_inc(m1_read, 1)
                elif name == "c2":
                    act.wait_ge(m1_full, rate_no(b, name))
                    f(c2T[:, :, :].rearrange("p g c -> p (g c)"), M1[:, 0:G * NC2], scale=SC1).then_inc(m1_read, 1)
                elif name == "pe":
                    act.wait_ge(m1_full, rate_no(b, name))
                    f(p2e[:, :], M1[0:H1 * NCA, 0:S]).then_inc(m1_read, 1)
                elif name == "zc":
                    act.wait_ge(m1_full, rate_no(b, name))
                    wait(act, z1_ready, G * (b.n - 1))
                    f(zc[p][:, :, :].rearrange("p g s -> p (g s)"), M1[:, :]).then_inc(m1_read, 1)

            def copy_u(b, g):
                act.wait_ge(pv_done, UNITS * b.n + (g + 1) * (UNITS // G))
                wait(act, fin_full, 3 * b.n)
                f(us[:, g, :], U[:, g * S:(g + 1) * S]).then_inc(u_read, 1)

            def step(prep, rate, att, fin):
                if fin:
                    copy_u(fin, 1)
                for n in range(UNITS + 1):
                    k = n - 1
                    if prep and k in prep.slots:
                        prep_piece(prep, prep.slots[k])
                    if prep and k == 1:
                        act.wait_ge(gz_ready, prep.n + 1)
                        f(gate[:, :], gz[:, :], ACT.Exp).then_inc(gz_exp, 1)
                    if prep and k == 9:
                        act.wait_ge(m0_read, prep_no(prep, "s2"))
                        e = e0[:, :, :].rearrange("p t n -> p (t n)")
                        f(e, e, ACT.Exp).then_inc(e0_exp, 1)
                    if rate and k in RATE_SLOT:
                        rate_piece(rate, RATE_SLOT[k])
                    if rate and k == 42:
                        act.wait_ge(m1_read, rate_no(rate, "sc"))
                        e = p2[:, :, :].rearrange("p h t -> p (h t)")
                        f(e, e, ACT.Exp).then_inc(s2_exp, 1)
                    if prep and prep.first and k == 40:
                        send_queries(act, prep)
                        for g in range(G):
                            load_parts(act, prep, g, qa, qscr, PARTS_Q)
                    if rate and prep and k == 33:
                        if not (isinstance(prep.n, int) and prep.n == B - 1):
                            act.wait_ge(m1_full, rate_no(rate, "v4"))
                            on_its_own(act)
                            act.wait_ge(res_ready, rate.n + 1)
                            on_its_own(act)
                            load_inputs(act, Batch(prep.i, prep.c + 1))
                    if att and k == 27:
                        copy_u(att, 0)
                    if att and n < UNITS:
                        act.wait_ge(st_full, UNITS * att.n + n + 1)
                        wait(act, pv_done, UNITS * att.n + n - NP + 1)
                        rows = P if unit(n)[1] < KT - 1 else LAST
                        f(pr[0:rows, n % NP, :], bank[n % ST][0:rows, :], ACT.Exp).then_inc(exp_done, 1)

            act.dma_start(wp[:, 0:NEARLY], w128[:, 0:NEARLY]).then_inc(w_loaded, 16)
            act.wait_ge(w_loaded, 32)
            act.dma_start(wp[:, NEARLY:], w128[:, NEARLY:]).then_inc(late_loaded, 16)
            act.wait_ge(ones_loaded, 32)
            steps(act, step)

        @block.vector
        def _(dve):
            dve.wait_ge(w_loaded, 32)
            mult, add, sub = ALU.mult, ALU.add, ALU.subtract

            def tt(o, a, b, op):
                return nc.vector.tensor_tensor(o, a, b, op)

            def prep_piece(b, name):
                p = b.par
                full = lambda: dve.wait_ge(m0_full, prep_no(b, name))
                if name == "small":
                    full()
                    lg = W("logits")
                    at = PREP_LINKS * b.n
                    nc.vector.tensor_scalar(gz[:, 0:1], M0[:, 352:353], 1.0 / T0, lg[:, 0:1], mult, add)\
                        .then_inc(prep_chain, 1)
                    for s in range(2):
                        tt(kb0a[:, s], M0[:, s * T0:(s + 1) * T0].unsqueeze(1).broadcast_to([P, HA, T0]),
                           W("mask_a").unsqueeze(2).broadcast_to([P, HA, T0]), mult)
                        tt(kb0b[:, s],
                           M0[0:32, 32 + s * T0:32 + (s + 1) * T0].unsqueeze(1).broadcast_to([32, HB, T0]),
                           W("mask_b", 32).unsqueeze(2).broadcast_to([32, HB, T0]), mult)
                    tt(vb0[:, :, :], M0[:, 64:320].rearrange("p (c n) -> p c n", c=4),
                       W("mask_v").unsqueeze(1).broadcast_to([P, 4, 64]), mult)
                    tt(vb4[:, :], M0[:, 320:352], W("mask_v4"), mult).then_inc(m0_read, 1)
                    dve.wait_ge(prep_chain, at + 1)
                    nc.vector.tensor_scalar(gz[:, 1:2], gz[:, 0:1], -1.0, lg[:, 2:3], mult, sub)\
                        .then_inc(prep_chain, 1)
                    dve.wait_ge(prep_chain, at + 2)
                    tt(gz[:, 0:1], gz[:, 0:1], lg[:, 1:2], sub).then_inc(gz_ready, 1)
                elif name[0] == "k":
                    dve.wait_ge(keys_full, keys_no(b, name))
                    n = int(name[-1])
                    at = KEYS.index(name)
                    dve.wait_ge(k1_ready, len(KEYS) * b.n + at + 1)
                    wait(dve, ksp_ready, len(KEYS) * b.n + at - 1)
                    first = kspa[:, 0, n * CH:(n + 1) * CH] if len(name) == 2 else kspb[:, 0, n, :]
                    rows = SPLIT_A if len(name) == 2 else P
                    tt(kr[0:rows, at % 2, :], keys_bank(b, name)[0:rows, 0:CH], first, sub)\
                        .then_inc(keys_read, 1)
                elif name in ("s0", "s1", "s2"):
                    full()
                    wait(dve, qsp_ready, b.n)
                    n = int(name[1])
                    wait(dve, m0_read, NPREP * (b.n - 1) + PREP.index("t2") + 1)
                    if n < 2:
                        src = M0[:, :].rearrange("p (g k) -> p g k", k=T0)
                        dst = e0[:, n, 0:512].rearrange("p (g k) -> p g k", k=T0)
                        m = m0x[:, n, 0:2 * HA]
                        mb = m.unsqueeze(2).broadcast_to([P, 2 * HA, T0])
                    else:
                        src = M0[:, 0:256].rearrange("p (t g k) -> p t g k", t=QT, k=T0)
                        dst = e0[:, :, 512:640].rearrange("p t (g k) -> p t g k", k=T0)
                        m = m0x[:, :, 2 * HA:2 * H0]
                        mb = m.unsqueeze(3).broadcast_to([P, QT, 2 * HB, T0])
                    nc.vector.reduce_max(m, src, AX.X).then_inc(prep_chain, 1)
                    dve.wait_ge(prep_chain, PREP_LINKS * b.n + 5 + n)
                    tt(dst, src, mb, sub).then_inc(m0_read, 1)
                elif name == "h":
                    full()
                    for g in range(G):
                        last = nc.vector.scalar_tensor_tensor(out=hT[p][:, g, :], in0=M0[:, g * S:(g + 1) * S],
                                                              scalar=W("b0p")[:, g:g + 1], in1=hT[p][:, g, :],
                                                              op0=add, op1=add)
                    last.then_inc(m0_read, 1)

            def rate_piece(b, name):
                p = b.par
                full = lambda: dve.wait_ge(m1_full, rate_no(b, name))
                base = RATE_LINKS * b.n
                if name == "ca":
                    full()
                    for g in range(G):
                        tt(k2b[:, g], M1[:, g * NCA:(g + 1) * NCA].unsqueeze(1).broadcast_to([P, HG, NCA]),
                           W("mask_h").unsqueeze(2).broadcast_to([P, HG, NCA]), mult)
                    tt(v2b[:, :], M1[0:H1 * NCA, S:2 * S], W("mask_v2", H1 * NCA), mult).then_inc(m1_read, 1)
                elif name[:2] == "cs":
                    full()
                    n = int(name[2])
                    nc.vector.tensor_reduce(cm[:, 2 * n:2 * n + 2], M1[:, :].rearrange("p (h s) -> p h s", h=2),
                                            AX.X, ALU.max, negate=True).then_inc(cm_ready, 1)
                elif name == "sc":
                    full()
                    s = M1[0:NC2, 0:H1 * NCA].rearrange("p (h t) -> p h t", h=H1)
                    nc.vector.reduce_max(m2[:, :], s, AX.X).then_inc(rate_chain, 1)
                    dve.wait_ge(rate_chain, base + 4)
                    tt(p2[:, :, :], s, m2[:, :].unsqueeze(2).broadcast_to([NC2, H1, NCA]), sub).then_inc(m1_read, 1)
                elif name in ("m0", "m1"):
                    g = int(name[1])
                    full()
                    wait(dve, mscr_done, 16 * (G * b.n + g))
                    at = base + (1, 7)[g]
                    m = M1[0:HG * QT, 0:P]
                    nc.vector.tensor_copy(msp[:, 0, :], m).then_inc(rate_chain, 1)
                    dve.wait_ge(rate_chain, at + 1)
                    tt(mr[:, :], m, msp[:, 0, :], sub).then_inc(m1_read, 1)
                    dve.wait_ge(m1_read, rate_no(b, name))
                    nc.vector.tensor_copy(msp[:, 1, :], mr[:, :]).then_inc(rate_chain, 1)
                    dve.wait_ge(rate_chain, at + 2)
                    tt(msp[:, 2, :], mr[:, :], msp[:, 1, :], sub).then_inc(msp_ready, 1)

            def group_max(b, g):
                n = HG * QT
                dve.wait_ge(sx_read, NMAX * b.n + (g + 1) * n * NCH)
                nc.vector.tensor_reduce(nm[:, g * n:(g + 1) * n], mx[:, g * n:(g + 1) * n, :], AX.X, ALU.max,
                                        negate=True).then_inc(rate_chain, 1)

            def sum_severity(b):
                dve.wait_ge(in_loaded[b.par], 48 * (b.half + 1))
                nc.vector.reduce_sum(sev[:, :], cT[b.par][:, 0:T0], AX.X).then_inc(sev_ready, 1)

            def step(prep, rate, att, fin):
                for k in range(UNITS):
                    if prep and prep.slots.get(k - 1) in KEYS:
                        prep_piece(prep, prep.slots[k - 1])
                    if prep and prep.slots.get(k, KEYS[0]) not in KEYS:
                        prep_piece(prep, prep.slots[k])
                    if prep and prep.first and prep.slots.get(k - 1) == "q1":
                        split_queries(dve, nc.vector, prep)
                    if prep and k == 3:
                        dve.wait_ge(gz_exp, prep.n + 1)
                        nc.vector.tensor_scalar_add(gate[:, :], gate[:, :], 1.0).then_inc(prep_chain, 1)
                        dve.wait_ge(prep_chain, PREP_LINKS * prep.n + 3)
                        nc.vector.reciprocal(gate[:, :], gate[:, :]).then_inc(prep_chain, 1)
                    if prep and k in (10, 11):
                        t = k - 10
                        dve.wait_ge(e0_exp, prep.n + 1)
                        nc.vector.reduce_sum(d0[:, t, :], e0[:, t, :].rearrange("p (g k) -> p g k", k=T0), AX.X)\
                            .then_inc(prep_chain, 1)
                    if prep and k == 12:
                        dve.wait_ge(prep_chain, PREP_LINKS * prep.n + 9)
                        nc.vector.reciprocal(d0[:, :, :], d0[:, :, :]).then_inc(prep_chain, 1)
                        dve.wait_ge(prep_chain, PREP_LINKS * prep.n + 10)
                        for s in range(2):
                            for o, n in ((s * HA, HA), (2 * HA + s * HB, HB)):
                                nc.vector.tensor_scalar(d0[:, :, o:o + n], d0[:, :, o:o + n],
                                                        gate[:, s:s + 1], None, mult).then_inc(w0_ready, 1)
                    if prep and k == 46 and not (isinstance(prep.n, int) and prep.n == B - 1):
                        sum_severity(Batch(prep.i, prep.c + 1))
                    if rate and k == 24:
                        group_max(rate, 0)
                    if rate and k == 48:
                        group_max(rate, 1)
                    if rate and k in RATE_SLOT:
                        rate_piece(rate, RATE_SLOT[k])
                    if rate and k == 18:
                        dve.wait_ge(m1_read, rate_no(rate, "cs2"))
                        nc.vector.reciprocal(cm[:, :], cden[:, :]).then_inc(cden_ready, 1)
                    if rate and k == 44:
                        base = RATE_LINKS * rate.n + 4
                        dve.wait_ge(s2_exp, rate.n + 1)
                        dve.wait_ge(m1_read, rate_no(rate, "sc"))
                        nc.vector.reduce_sum(d2[:, :], p2[:, :, :], AX.X).then_inc(rate_chain, 1)
                        dve.wait_ge(rate_chain, base + 1)
                        nc.vector.reciprocal(d2[:, :], d2[:, :]).then_inc(rate_chain, 1)
                        dve.wait_ge(rate_chain, base + 2)
                        tt(p2[:, :, :], p2[:, :, :], d2[:, :].unsqueeze(2).broadcast_to([NC2, H1, NCA]), mult)\
                            .then_inc(p2_ready, 1)
                    for b, g, at in ((fin, 1, DEN1), (att, 0, DEN0)):
                        if b and k == at:
                            dve.wait_ge(fin_full, 3 * b.n + g + 1)
                            wait(dve, out_stored, 16 * b.n)
                            nc.vector.reciprocal(rb[:, g, :], M1[:, 0:S]).then_inc(fin_read, 1)
                    if fin and k == OUT:
                        dve.wait_ge(fin_full, 3 * fin.n + 3)
                        dve.wait_ge(res_ready, fin.n + 1)
                        tt(o1, M1[:, 0:QT * D],
                           res[fin.par][:, :, :].rearrange("p t d -> p (t d)"), add).then_inc(fin_read, 1)

                    if rate:
                        for h, t, c, n in chunks_of(k):
                            dve.wait_ge(sx_full, NMAX * rate.n + n + 1)
                            w = min(CH, NKEY - c * CH)
                            nc.vector.reduce_max(mx[:, h * QT + t, c:c + 1], SX[n % NX][:, 0:w], AX.X)\
                                .then_inc(sx_read, 1)

            sum_severity(Batch(0, 0))
            steps(dve, step)

        @block.gpsimd
        def _(pool):
            def tt(o, a, b, op):
                return nc.gpsimd.tensor_tensor(o, a, b, op)

            nc.gpsimd.memset(kspa[0:3, 0, :], 1.0).then_inc(consts, 1)
            for p in range(2):
                nc.gpsimd.memset(v[p][:, :, :, D1 + 1:PAD], 0.0)
                nc.gpsimd.memset(v[p][:, :, :, D1:D1 + 1], 1.0).then_inc(consts, 1)
            pool.wait_ge(w_loaded, 32)

            def split(b, name):
                at = KEYS.index(name)
                n = int(name[-1])
                if len(name) == 2:
                    rows, parts = SPLIT_A, [kspa[:, a, n * CH:(n + 1) * CH] for a in range(3)]
                else:
                    rows, parts = P, [kspb[:, a, n, :] for a in range(3)]
                pool.wait_ge(keys_read, keys_no(b, name))
                on_its_own(pool)
                nc.gpsimd.tensor_copy(parts[1], kr[0:rows, at % 2, :]).then_inc(split_chain, 1)
                pool.wait_ge(split_chain, len(KEYS) * b.n + at + 1)
                tt(parts[2], kr[0:rows, at % 2, :], parts[1], ALU.subtract).then_inc(ksp_ready, 1)

            def store_maxima(b, g):
                pool.wait_ge(msp_ready, G * b.n + g + 1)
                wait(pool, m_loaded[g], 16 * b.n)
                on_its_own(pool)
                pool.dma_start(mscr[g].rearrange("a r q -> r a q"), msp[:, :, :]).then_inc(mscr_done, 16)

            def load_maxima(b, g):
                pool.wait_ge(mscr_done, 16 * (G * b.n + g + 1))
                on_its_own(pool)
                pool.dma_start(qa[b.par][KR:KR + 3, g * HG:(g + 1) * HG, :],
                               mscr[g].rearrange("a (h t) q -> a h (t q)", t=QT)).then_inc(m_loaded[g], 16)

            def normalise(b, g):
                pool.wait_ge(fin_read, 3 * b.n + g + 1)
                tt(us[:, g, :], us[:, g, :], rb[:, g, :], ALU.mult).then_inc(z_chain, 1)
                pool.wait_ge(z_chain, G * b.n + g + 1)
                tt(us[:, g, :], us[:, g, :], zc[b.par][:, g, :], ALU.add).then_inc(z1_ready, 1)

            def repeat_tokens(b):
                pool.wait_ge(in_loaded[b.par], 48 * (b.half + 1))
                wait(pool, m0_full, NPREP * (b.n - 1) + 1)
                on_its_own(pool)
                for s, t in enumerate((T0, 0)):
                    last = nc.gpsimd.tensor_copy(
                        tok0[:, s], cT[b.par][:, t:t + T0].unsqueeze(1).broadcast_to([C, 8, T0]))
                last.then_inc(tok0_ready, 1)

            def step(prep, rate, att, fin):
                for slot in range(UNITS + 1):
                    k = slot - 1
                    if att and slot == 0:
                        load_maxima(att, 1)
                    if prep and k == 42:
                        wait(pool, m1_full, NRATE * (prep.n - 1) + RATE.index("ca") + 1)
                        on_its_own(pool)
                        nc.gpsimd.tensor_copy(tok2[:, :, :], cT[prep.par][:, NKEY:NCTX].unsqueeze(1)
                                              .broadcast_to([C, H1, NCA])).then_inc(tok2_ready, 1)
                    if prep and k == 46 and not (isinstance(prep.n, int) and prep.n == B - 1):
                        repeat_tokens(Batch(prep.i, prep.c + 1))
                    if fin and k == DEN1 + 1:
                        normalise(fin, 1)
                    if prep and prep.slots.get(k) in KEYS:
                        split(prep, prep.slots[k])
                    if prep and k == 12:
                        pool.wait_ge(w0_ready, 4 * (prep.n + 1))
                        e = e0[:, :, :].rearrange("p t (g k) -> p t g k", k=T0)
                        tt(e, e, d0[:, :, :].unsqueeze(3).broadcast_to([P, QT, 2 * H0, T0]), ALU.mult)\
                            .then_inc(p0_ready, 1)
                    if prep and not prep.first and prep.slots.get(k) == "q1":
                        split_queries(pool, nc.gpsimd, prep)
                    if rate and k == 16:
                        pool.wait_ge(m0_read, prep_no(rate, "hn"))
                        wait(pool, fin_read, 3 * (rate.n - 1))
                        for t in range(QT):
                            last = tt(res[rate.par][:, t, :].rearrange("p (h d) -> p h d", d=D1),
                                      hn[rate.par][:, t, :].rearrange("p (h d) -> p h d", d=PAD)[:, :, 0:D1],
                                      W("b1n").rearrange("p (h d) -> p h d", d=D1), ALU.add)
                        last.then_inc(res_ready, 1)
                    if rate and k == 5:
                        pool.wait_ge(m1_read, rate_no(rate, "caq"))
                        for g in range(G):
                            last = tt(caqb[:, g], caq[:, g, :].unsqueeze(1).broadcast_to([P, HG, NC2]),
                                      W("mask_h").unsqueeze(2).broadcast_to([P, HG, NC2]), ALU.mult)
                        last.then_inc(caqb_ready, 1)
                    if rate and k == 19:
                        pool.wait_ge(cden_ready, rate.n + 1)
                        tt(pc[:, :, :], pc[:, :, :], cm[:, :].unsqueeze(2).broadcast_to([P, CT, S]), ALU.mult)\
                            .then_inc(pc_ready, 1)
                    if rate and k == 29:
                        store_maxima(rate, 0)
                    if rate and k == 34:
                        load_maxima(rate, 0)
                    if att and k == DEN0 + 1:
                        normalise(att, 0)
                if rate:
                    store_maxima(rate, 1)

            repeat_tokens(Batch(0, 0))
            steps(pool, step)


def kernel(x, ctx_768, L0_xattn_w_q, L0_xattn_w_k, L0_xattn_w_v, L0_xattn_w_k_dis, L0_xattn_w_v_dis,
           L0_xattn_w_gate, L0_xattn_b_gate, L0_xattn_anat_gate_logit, L0_xattn_dis_gate_logit,
           L0_xattn_w_out, L0_xattn_b_out, L1_xattn_Wq, L1_xattn_Wk, L1_xattn_Wv, L1_xattn_Wq_ca,
           L1_xattn_Wk_ca, L1_xattn_Wv_ca, L1_xattn_Wout, L1_xattn_b_out):
    import concourse.bacc as bacc
    from concourse.bass_utils import run_bass_kernel_spmd

    def cols(a):
        a = np.asarray(a)
        out = np.zeros((*a.shape[:-1], G, HG, PAD), a.dtype)
        out[..., :D1] = a.reshape(*a.shape[:-1], G, HG, D1)
        return out.reshape(*a.shape[:-1], G * P)

    def rows(a):
        return cols(np.asarray(a).T).reshape(-1, G, P).transpose(2, 1, 0)

    def table(n, widths, at, items):
        out = np.zeros((n, sum(widths.values())), np.float32)
        for name, a in items.items():
            a = np.asarray(a)
            a = a.reshape(a.shape[0], -1)
            out[:a.shape[0], at[name][0]:at[name][0] + a.shape[1]] = a
        return out

    r = np.arange(P)
    same = lambda a, b: (a[:, None] == b[None, :])
    wo0 = cols(np.asarray(L0_xattn_w_out).T)
    wq1 = rows(L1_xattn_Wq)
    all_rows = lambda a: np.broadcast_to(np.asarray(a), (P, np.size(a)))
    items = dict(
        ident=np.eye(P), b0p=cols(L0_xattn_b_out).reshape(G, P).T,
        b1n=all_rows(L1_xattn_b_out),
        spread=(r[:, None] % PAD == D1) & same(r // PAD, r // PAD),
        mask_a=same(r // D0, np.arange(HA)), mask_b=same(r[:HB * D0] // D0, np.arange(HB)),
        mask_h=same(r // PAD, np.arange(HG)), mask_v=same(r // T0, np.arange(64) // D0),
        mask_v4=same(r % 64 // T0, np.arange(32) // D0),
        logits=np.stack([np.broadcast_to(np.asarray(a).reshape(()), (P,)) for a in (
            L0_xattn_b_gate, L0_xattn_anat_gate_logit, L0_xattn_dis_gate_logit)], 1),
        wq0=rows(np.asarray(L0_xattn_w_q).T), wo0a=wo0[:P], wo0b=wo0[P:],
        wq1=np.concatenate([wq1, np.zeros((P, G, 2 * SPLIT_A - D), np.float32)], 2),
        wqpp=cols(wq1), wo1=rows(L1_xattn_Wout),
        mask_v2=same(np.arange(H1 * NCA) // NCA, np.arange(G * P) // PAD))
    w128 = table(P, W128, O128, items)
    repeat = np.linspace(0, NC2 - 1, S).astype(np.int64)
    items = dict(
        wk0=np.asarray(L0_xattn_w_k).T, wkd0=np.asarray(L0_xattn_w_k_dis).T,
        wv0=np.asarray(L0_xattn_w_v).T, wvd0=np.asarray(L0_xattn_w_v_dis).T,
        wg=np.asarray(L0_xattn_w_gate).T, repeat=same(np.arange(NC2), repeat),
        wk1=L1_xattn_Wk, wv1=L1_xattn_Wv, wkca=cols(L1_xattn_Wk_ca), wvca=cols(L1_xattn_Wv_ca),
        wqca=cols(L1_xattn_Wq_ca))
    w96 = table(C, W96, O96, items)
    xp = cols(x)
    c = np.asarray(ctx_768)
    arrays = {
        "x_t": xp.reshape(B, S, G, P).transpose(0, 3, 2, 1),
        "ctx_t": c.transpose(0, 2, 1), "ca_n": c[:, NKEY:], "w128": w128, "w96": w96,
    }
    arrays = {n: np.ascontiguousarray(a) for n, a in arrays.items()}
    nc = bacc.Bacc("TRN2", target_bir_lowering=False, num_devices=1)
    aps = [nc.dram_tensor(n, a.shape, mybir.dt.from_np(a.dtype), kind="ExternalInput").ap()
           for n, a in arrays.items()]
    out = nc.dram_tensor("out", (B, S, D), mybir.dt.float32, kind="ExternalOutput").ap()
    program(nc, *aps, out)
    return run_bass_kernel_spmd(nc, [arrays], core_ids=[0]).results[0]["out"]
```
